# Optimizing a Trainium2 kernel written in Bass

```python
import numpy as np
import jax
import jax.numpy as jnp

def _softmax(x, axis=-1):
    return jax.nn.softmax(x, axis=axis)

def _gelu(x):
    return jax.nn.gelu(x, approximate=True)

def _silu(x):
    return jax.nn.silu(x)

def _sigmoid(x):
    return jax.nn.sigmoid(x)

def _layernorm(x, axis=-1, eps=1e-05):
    m = jnp.mean(x, axis=axis, keepdims=True)
    v = jnp.var(x, axis=axis, keepdims=True)
    return (x - m) / jnp.sqrt(v + eps)

def _scatter_add(tgt, idx, src, axis=0):
    return tgt.at[idx].add(src)

def _segment_sum(src, seg, n):
    return jax.ops.segment_sum(src, seg, n)
kernel_name = 'mk_decoder_preln_d1_seqx_r4_d7a771'

def setup_inputs(seed: int=0):
    np.random.seed(seed)
    _w = jnp.asarray

    def _rec_inputs():
        import jax
        import jax.numpy as jnp
        _rk = jax.random.key(seed)
        x = 0.0002417 + 0.9998 * jax.random.normal(jax.random.fold_in(_rk, 1), (8, 256, 256), jnp.float32)
        _lenS = 256 - jax.random.randint(jax.random.fold_in(_rk, 7), (8,), 0, max(1, 256 // 4) + 1, jnp.int32)
        _lenS2 = 256 - jax.random.randint(jax.random.fold_in(_rk, 8), (8,), 0, max(1, 256 // 4) + 1, jnp.int32)
        _ctx_1024P = jax.random.normal(jax.random.fold_in(_rk, 11), (8, 16, 256), jnp.float32)
        _ctx_1024c = jax.random.dirichlet(jax.random.fold_in(_rk, 511), 0.3 * jnp.ones((16,), jnp.float32), (8, 256))
        _ctx_1024t = jnp.einsum('bsk,bkd->bsd', _ctx_1024c, _ctx_1024P)
        _ctx_1024t = _ctx_1024t * jax.lax.rsqrt(jnp.mean(jnp.square(_ctx_1024t)) + 1e-12) * 0.953939
        ctx_1024 = 7.22013e-05 + 1.00017 * (_ctx_1024t + 0.3 * jax.random.normal(jax.random.fold_in(_rk, 611), (8, 256, 256), jnp.float32))
        _validS = jnp.arange(256)[None, :] < _lenS[:, None]
        _validS2 = jnp.arange(256)[None, :] < _lenS2[:, None]
        _causal = jnp.tril(jnp.ones((256, 256), dtype=bool))
        mask_Bx1x1xS2_ik0 = jnp.where(jnp.broadcast_to(_validS2[:, None, None, :], (8, 1, 1, 256)), 0, 1).astype(jnp.int32)
        return (x, ctx_1024, mask_Bx1x1xS2_ik0)
    x, ctx_1024, mask_Bx1x1xS2_ik0 = _rec_inputs()

    def _L0_attn_setup():
        import jax, jax.numpy as jnp
        import numpy as np
        H = 16
        GRID = 16
        TOK_PER_FRAME = GRID * GRID

        def _rope(x, pos, dim):
            half = dim // 2
            omega = jnp.arange(half, dtype=x.dtype) / (dim / 2.0)
            inv = 1.0 / 10000.0 ** omega
            freq = pos.astype(x.dtype)[:, None] * inv
            sin = jnp.concatenate([jnp.sin(freq), jnp.sin(freq)], axis=-1)
            cos = jnp.concatenate([jnp.cos(freq), jnp.cos(freq)], axis=-1)
            y = x.reshape(*x.shape[:-1], half, 2)
            y1, y2 = (y[..., 0], y[..., 1])
            rot = jnp.stack((-y2, y1), axis=-1).reshape(x.shape)
            return x * cos + rot * sin

        def _apply_3d_rope(qk, f_ids, h_ids, w_ids, d_dim):
            s = 0
            parts = []
            for pos in (f_ids, h_ids, w_ids):
                parts.append(_rope(qk[..., s:s + d_dim], pos, d_dim))
                s += d_dim
            if s < qk.shape[-1]:
                parts.append(qk[..., s:])
            return jnp.concatenate(parts, axis=-1)
        key = jax.random.key(seed)
        ks = jax.random.split(key, 5)
        D = 256
        B, N = (4, 512)
        sc = 0.02
        return {'hidden_states': jax.random.normal(ks[0], (B, N, D), jnp.float32), 'Wq': jax.random.normal(ks[1], (D, D), jnp.float32) * sc, 'bq': jnp.zeros((D,), jnp.float32), 'Wk': jax.random.normal(ks[2], (D, D), jnp.float32) * sc, 'bk': jnp.zeros((D,), jnp.float32), 'Wv': jax.random.normal(ks[3], (D, D), jnp.float32) * sc, 'bv': jnp.zeros((D,), jnp.float32), 'Wo': jax.random.normal(ks[4], (D, D), jnp.float32) * sc, 'bo': jnp.zeros((D,), jnp.float32)}
    _L0_attn_all = _L0_attn_setup()
    _L0_attn_in = {k: v for k, v in _L0_attn_all.items() if k in ('Wq', 'bq', 'Wk', 'bk', 'Wv', 'bv', 'Wo', 'bo')}
    del _L0_attn_all

    def _L0_xattn_setup():
        import jax, jax.numpy as jnp
        import numpy as np
        HEADS = 16
        EMBED = 256
        NEG = -1e+20
        key = jax.random.key(seed)
        k1, k2, k3, k4, k5 = jax.random.split(key, 5)
        N, S, E = (4, 512, EMBED)
        values = jax.random.normal(k1, (N, S, E), dtype=jnp.float32)
        keys = jax.random.normal(k2, (N, S, E), dtype=jnp.float32)
        query = jax.random.normal(k3, (N, S, E), dtype=jnp.float32)
        mask = jax.random.randint(k4, (N, 1, 1, S), 0, 2, dtype=jnp.int32)
        W_fc = jax.random.normal(k5, (E, E), dtype=jnp.float32) * (1.0 / np.sqrt(E))
        return {'values': values, 'keys': keys, 'query': query, 'mask': mask, 'W_fc': W_fc}
    _L0_xattn_all = _L0_xattn_setup()
    _L0_xattn_in = {k: v for k, v in _L0_xattn_all.items() if k in ('W_fc',)}
    del _L0_xattn_all

    def _L0_ffn_setup():
        import jax, jax.numpy as jnp
        import numpy as np
        NUM_EXPERTS = 8
        NUM_LANGS = 4
        TOP_K = 2
        D_MODEL = 256
        EXPERT_SIZE = 1024
        B, S = (2, 512)
        key = jax.random.key(seed)
        ks = jax.random.split(key, 6)

        def xavier(k, shape, fan_in, fan_out):
            a = float(np.sqrt(6.0 / (fan_in + fan_out)))
            return jax.random.uniform(k, shape, jnp.float32, -a, a)
        return {'x': jax.random.normal(ks[0], (B, S, D_MODEL), jnp.float32), 'router_w': xavier(ks[1], (NUM_EXPERTS, D_MODEL), D_MODEL, NUM_EXPERTS), 'router_b': jnp.zeros((NUM_EXPERTS,), jnp.float32), 'lang_w': xavier(ks[2], (NUM_LANGS, D_MODEL), D_MODEL, NUM_LANGS), 'lang_b': jnp.zeros((NUM_LANGS,), jnp.float32), 'w1': xavier(ks[3], (NUM_EXPERTS, D_MODEL, EXPERT_SIZE), D_MODEL, EXPERT_SIZE), 'b1': jnp.zeros((NUM_EXPERTS, EXPERT_SIZE), jnp.float32), 'w2': xavier(ks[4], (NUM_EXPERTS, EXPERT_SIZE, D_MODEL), EXPERT_SIZE, D_MODEL), 'b2': jnp.zeros((NUM_EXPERTS, D_MODEL), jnp.float32)}
    _L0_ffn_all = _L0_ffn_setup()
    _L0_ffn_in = {k: v for k, v in _L0_ffn_all.items() if k in ('router_w', 'router_b', 'lang_w', 'lang_b', 'w1', 'b1', 'w2', 'b2')}
    del _L0_ffn_all
    return {'x': x, 'ctx_1024': ctx_1024, 'mask_Bx1x1xS2_ik0': mask_Bx1x1xS2_ik0, 'L0_attn_Wq': _L0_attn_in['Wq'], 'L0_attn_bq': _L0_attn_in['bq'], 'L0_attn_Wk': _L0_attn_in['Wk'], 'L0_attn_bk': _L0_attn_in['bk'], 'L0_attn_Wv': _L0_attn_in['Wv'], 'L0_attn_bv': _L0_attn_in['bv'], 'L0_attn_Wo': _L0_attn_in['Wo'], 'L0_attn_bo': _L0_attn_in['bo'], 'L0_xattn_W_fc': _L0_xattn_in['W_fc'], 'L0_ffn_router_w': _L0_ffn_in['router_w'], 'L0_ffn_router_b': _L0_ffn_in['router_b'], 'L0_ffn_lang_w': _L0_ffn_in['lang_w'], 'L0_ffn_lang_b': _L0_ffn_in['lang_b'], 'L0_ffn_w1': _L0_ffn_in['w1'], 'L0_ffn_b1': _L0_ffn_in['b1'], 'L0_ffn_w2': _L0_ffn_in['w2'], 'L0_ffn_b2': _L0_ffn_in['b2']}

def reference(x, ctx_1024, mask_Bx1x1xS2_ik0, L0_attn_Wq, L0_attn_bq, L0_attn_Wk, L0_attn_bk, L0_attn_Wv, L0_attn_bv, L0_attn_Wo, L0_attn_bo, L0_xattn_W_fc, L0_ffn_router_w, L0_ffn_router_b, L0_ffn_lang_w, L0_ffn_lang_b, L0_ffn_w1, L0_ffn_b1, L0_ffn_w2, L0_ffn_b2):
    import jax
    import jax.numpy as jnp

    def _L0_attn_ref(hidden_states, Wq, bq, Wk, bk, Wv, bv, Wo, bo):
        import jax, jax.numpy as jnp
        import numpy as np
        H = 16
        GRID = 16
        TOK_PER_FRAME = GRID * GRID

        def _rope(x, pos, dim):
            half = dim // 2
            omega = jnp.arange(half, dtype=x.dtype) / (dim / 2.0)
            inv = 1.0 / 10000.0 ** omega
            freq = pos.astype(x.dtype)[:, None] * inv
            sin = jnp.concatenate([jnp.sin(freq), jnp.sin(freq)], axis=-1)
            cos = jnp.concatenate([jnp.cos(freq), jnp.cos(freq)], axis=-1)
            y = x.reshape(*x.shape[:-1], half, 2)
            y1, y2 = (y[..., 0], y[..., 1])
            rot = jnp.stack((-y2, y1), axis=-1).reshape(x.shape)
            return x * cos + rot * sin

        def _apply_3d_rope(qk, f_ids, h_ids, w_ids, d_dim):
            s = 0
            parts = []
            for pos in (f_ids, h_ids, w_ids):
                parts.append(_rope(qk[..., s:s + d_dim], pos, d_dim))
                s += d_dim
            if s < qk.shape[-1]:
                parts.append(qk[..., s:])
            return jnp.concatenate(parts, axis=-1)
        B, N, D = hidden_states.shape
        hd = D // H
        d_dim = 2 * (hd // 3 // 2)

        def heads(x):
            return x.reshape(B, N, H, hd).transpose(0, 2, 1, 3)
        q = heads(hidden_states @ Wq + bq)
        k = heads(hidden_states @ Wk + bk)
        v = heads(hidden_states @ Wv + bv)
        ids = jnp.arange(N)
        f_ids = ids // TOK_PER_FRAME
        rem = ids - TOK_PER_FRAME * f_ids
        h_ids = rem // GRID
        w_ids = rem - GRID * h_ids
        q = _apply_3d_rope(q, f_ids, h_ids, w_ids, d_dim)
        k = _apply_3d_rope(k, f_ids, h_ids, w_ids, d_dim)
        scale = hd ** (-0.5)
        attn = jnp.einsum('bhqd,bhkd->bhqk', q, k) * scale
        attn = jax.nn.softmax(attn.astype(jnp.float32), axis=-1).astype(q.dtype)
        ctx = jnp.einsum('bhqk,bhkd->bhqd', attn, v)
        ctx = ctx.transpose(0, 2, 1, 3).reshape(B, N, D)
        return ctx @ Wo + bo

    def _L0_xattn_ref(values, keys, query, mask, W_fc):
        import jax, jax.numpy as jnp
        import numpy as np
        HEADS = 16
        EMBED = 256
        NEG = -1e+20
        N, Q, E = query.shape
        H = HEADS
        D = E // H
        q = query.reshape(N, Q, H, D)
        k = keys.reshape(N, keys.shape[1], H, D)
        v = values.reshape(N, values.shape[1], H, D)
        energy = jnp.einsum('nqhd,nkhd->nhqk', q, k)
        energy = jnp.where(mask == 0, jnp.float32(NEG), energy)
        attention = jax.nn.softmax(energy * (1.0 / np.sqrt(E)), axis=-1)
        out = jnp.einsum('nhqk,nkhd->nqhd', attention, v).reshape(N, Q, E)
        return out @ W_fc.T

    def _L0_ffn_ref(x, router_w, router_b, lang_w, lang_b, w1, b1, w2, b2):
        import jax, jax.numpy as jnp
        import numpy as np
        NUM_EXPERTS = 8
        NUM_LANGS = 4
        TOP_K = 2
        D_MODEL = 256
        EXPERT_SIZE = 1024
        B, S = (2, 512)
        lang_logits = x @ lang_w.T + lang_b
        lang_probs = jax.nn.softmax(lang_logits, axis=-1)
        lp_pad = jnp.pad(lang_probs, ((0, 0), (0, 0), (0, 1)))
        idx = jnp.arange(NUM_EXPERTS) % NUM_LANGS
        expert_weights = lp_pad[..., idx] + lp_pad[..., idx + 1]
        router_logits = x @ router_w.T + router_b + 0.1 * expert_weights
        router_probs = jax.nn.softmax(router_logits, axis=-1)
        top_p, top_i = jax.lax.top_k(router_probs, TOP_K)
        top_p = top_p / top_p.sum(axis=-1, keepdims=True)
        h = jax.nn.gelu(jnp.einsum('bsd,edh->bseh', x, w1) + b1, approximate=False)
        expert_out = jnp.einsum('bseh,ehd->bsed', h, w2) + b2
        sel = jnp.take_along_axis(expert_out, top_i[..., None], axis=2)
        return (top_p[..., None] * sel).sum(axis=2)
    x = x + _L0_attn_ref(_layernorm(x, axis=-1), L0_attn_Wq, L0_attn_bq, L0_attn_Wk, L0_attn_bk, L0_attn_Wv, L0_attn_bv, L0_attn_Wo, L0_attn_bo)
    x = x + _L0_xattn_ref(ctx_1024, ctx_1024, _layernorm(x, axis=-1), mask_Bx1x1xS2_ik0, L0_xattn_W_fc)
    x = x + _L0_ffn_ref(_layernorm(x, axis=-1), L0_ffn_router_w, L0_ffn_router_b, L0_ffn_lang_w, L0_ffn_lang_b, L0_ffn_w1, L0_ffn_b1, L0_ffn_w2, L0_ffn_b2)
    return x

_drawn_inputs = setup_inputs


def setup_inputs(seed=0):
    import zlib

    import numpy as np

    out = dict(_drawn_inputs(seed))
    spreads = {'L0_attn_bq': (0.0, 0.8),
     'L0_attn_bk': (0.0, 0.8),
     'L0_attn_bv': (0.0, 0.1),
     'L0_attn_bo': (0.0, 0.1),
     'L0_ffn_router_b': (0.0, 0.1),
     'L0_ffn_lang_b': (0.0, 2.0),
     'L0_ffn_b1': (0.0, 0.1),
     'L0_ffn_b2': (0.0, 0.1)}
    factors = {'L0_attn_Wq': 8.0, 'L0_attn_Wk': 6.596, 'L0_attn_Wv': 4.097}
    for name, (base, spread) in spreads.items():
        noise = np.random.default_rng([zlib.crc32(name.encode()), seed]).standard_normal(out[name].shape)
        drawn = base * np.exp(spread * noise) if base else spread * noise
        out[name] = jnp.asarray(drawn.astype(out[name].dtype))
    for name, factor in factors.items():
        out[name] = (out[name] * factor).astype(out[name].dtype)
    return out
```

```python
from contextlib import ExitStack

import numpy as np

import concourse.bass as bass
from concourse import mybir

F32 = mybir.dt.float32
BF16 = mybir.dt.bfloat16
I32 = mybir.dt.int32
U32 = mybir.dt.uint32
ALU = mybir.AluOpType
ACT = mybir.ActivationFunctionType
AXX = mybir.AxisListType.X

P = 128
B, S, D = 8, 256, 256
H, HD = 16, 16
T = S // P
KC = D // P
NT = B * T
PARTS = 3
Q_PARTS = (0, 0, 0, 1, 1, 2)
K_PARTS = (0, 1, 2, 0, 1, 0)
STACK = 6 * HD
MASK0 = STACK
MAX0 = STACK + PARTS
ROWS = STACK + 2 * PARTS
VW = 32
BANK = 512
MAX_PARTS = 5
NEG = -1e20
EPS = 1e-5
E, L, TOPK, F = 8, 4, 2, 1024
FC = F // P
N_TILES = (NT * P * TOPK - E) // P + E
RSQRT_MAGIC = 0x5F3759DF


def bf16_parts(value):
    rest, out = np.array([value], np.float32), []
    for _ in range(PARTS):
        part = (rest.view(np.uint32) & np.uint32(0xFFFF0000)).view(np.float32)
        out.append(float(part[0]))
        rest = rest - part
    return out


class Steps:

    def __init__(self, sem, per_pass, credit=0, by=1):
        self.sem, self.per_pass, self.credit, self.by, self.k = sem, per_pass, credit, by, 0

    def start(self):
        self.k = 0

    def end(self):
        assert self.k == self.per_pass, (self.sem.name, self.k, self.per_pass)

    def done(self, instruction):
        self.k += 1
        instruction.then_inc(self.sem, self.by)
        return self.k

    def wait(self, engine, n, k=None):
        k = self.k if k is None else k
        engine.wait_ge(self.sem, (n * self.per_pass + k) * self.by + self.credit)

    def hold(self, engine, n, k=None, idle=None):
        self.wait(engine, n, k)
        engine.sem_inc(idle, 1)


class Slots:

    def __init__(self, full, free, banks, fills_per_pass):
        per_pass = [(fills_per_pass + 1) // 2, fills_per_pass // 2]
        self.full = [Steps(s, k) for s, k in zip(full, per_pass)]
        self.free = [Steps(s, k, credit=1) for s, k in zip(free, per_pass)]
        self.banks, self.unit = banks, 0

    def prime(self, nc):
        for s in self.free:
            nc.vector.sem_inc(s.sem, 1)

    def start(self):
        self.unit = 0
        for s in self.full + self.free:
            s.start()

    def end(self):
        for s in self.full + self.free:
            s.end()

    def fill(self, pe, n):
        i = self.unit % 2
        self.unit += 1
        self.free[i].wait(pe, n)
        return i, self.banks[i]

    def filled(self, i, instruction):
        self.full[i].done(instruction)

    def take(self, engine, n, i):
        self.full[i].wait(engine, n)

    def taken(self, i, instruction):
        return self.free[i], self.free[i].done(instruction)


def layer_norm(nc, n, dve, src, dst, st):
    v = nc.vector
    for t in range(T):
        dve.done(v.bn_stats(st["bn"][:, t, :], src[:, t, :]))
    dve.hold(v, n, idle=st["idle"])
    for t in range(T):
        dve.done(v.bn_aggr(st["mv"][:, t, :], st["bn"][:, t, :]))
    dve.wait(v, n)
    var, y, w = st["var"][:, :], st["rstd"][:, :], st["tmp"][:, :]
    dve.done(v.tensor_scalar(var, st["mv"][:, :, 1], EPS, None, ALU.add))
    dve.wait(v, n)
    dve.done(v.tensor_scalar(w.bitcast(I32), var.bitcast(I32), 1, None, ALU.logical_shift_right))
    dve.wait(v, n)
    dve.done(v.tensor_scalar(y.bitcast(I32), w.bitcast(I32), -1, float(RSQRT_MAGIC), ALU.mult, ALU.add))
    for _ in range(4):
        dve.wait(v, n)
        dve.done(v.tensor_tensor(w, y, y, ALU.mult))
        dve.wait(v, n)
        dve.done(v.scalar_tensor_tensor(out=w, in0=w, scalar=-0.5, in1=var, op0=ALU.mult, op1=ALU.mult))
        dve.wait(v, n)
        dve.done(v.scalar_tensor_tensor(out=y, in0=w, scalar=1.5, in1=y, op0=ALU.add, op1=ALU.mult))
    dve.wait(v, n)
    for t in range(T):
        k = dve.done(v.tensor_scalar(dst[:, t, :], src[:, t, :], st["mv"][:, t, 0:1], y[:, t:t + 1],
                                     ALU.subtract, ALU.mult))
    return k


class Attention:

    def __init__(self, nc, ctx, name, ident, identb, scale, steps):
        self.nc, self.name, self.scale, self.ident, self.identb = nc, name, scale, ident, identb

        def sb(what, shape, dt=F32):
            return ctx.enter_context(nc.sbuf_tensor(f"{name}_{what}", shape, dt))

        def sem(what):
            return ctx.enter_context(nc.semaphore(f"{name}_{what}"))

        self.psum = ctx.enter_context(nc.psum_tensor(f"{name}_psum", [P, 4, BANK], F32))
        self.slots = Slots([sem("full0"), sem("full1")], [sem("free0"), sem("free1")],
                           [self.psum[:, 0, :], self.psum[:, 1, :]], steps["fills"])
        self.o_psum = self.psum[:, 2:4, :]
        self.dve = Steps(sem("dve"), steps["dve"])
        self.act = Steps(sem("act"), steps["act"])
        self.pool = Steps(sem("pool"), steps["pool"])
        self.pv = Steps(sem("pv"), H)
        self.max_dma = Steps(sem("max_dma"), PARTS, by=16)
        self.all = [self.slots, self.dve, self.act, self.pool, self.pv, self.max_dma]

        self.stats = {"bn": sb("bn", [P, T, 6]), "mv": sb("mv", [P, T, 2]), "var": sb("var", [P, T]),
                      "rstd": sb("rstd", [P, T]), "tmp": sb("tmp", [P, T]), "idle": sem("idle_dve")}
        self.idle_pool = sem("idle_pool")
        self.xn = sb("xn", [P, T, D])
        self.xnT = sb("xnT", [P, KC, T, P])
        self.rest = sb("rest", [P, 2, T, D])
        self.parts = [sb(f"parts_{w}", [P, T, H, ROWS], BF16) for w in "qk"]
        self.stack = [sb(f"stack_{w}", [ROWS, H, T, P], BF16) for w in "qk"]
        self.v = sb("v", [P, T, H, VW])
        self.neg_max = sb("neg_max", [P, T, H])
        self.max_rest = sb("max_rest", [P, T, H])
        self.max_parts = sb("max_parts", [P, T, MAX_PARTS, H], BF16)
        self.maxT = sb("maxT", [PARTS * H, T, P], BF16)
        self.p = sb("p", [P, 2, BANK])
        self.oT = self.rest[:, :, :, :].rearrange("p w t d -> p (w t) d")
        self.rden = sb("rden", [P, T, H])
        self.ctx, self.ctxT = self.xn, self.xnT

    def setup(self, count):
        nc = self.nc
        q, k = self.parts
        count.done(nc.gpsimd.memset(self.max_parts[:, :, :, :], 0.0))
        for what, value in ((q[:, :, :, MASK0:MAX0], 1.0), (q[:, :, :, MAX0:ROWS], 0.0),
                            (k[:, :, :, MASK0:MAX0], 0.0), (k[:, :, :, MAX0:ROWS], 1.0),
                            (self.v[:, :, :, HD:HD + 1], 1.0), (self.v[:, :, :, HD + 1:VW], 0.0)):
            count.done(nc.gpsimd.memset(what, value))

    def start(self):
        for s in self.all:
            s.start()

    def end(self):
        for s in self.all:
            s.end()

    def turn_rows(self, n, rows, turned, ready):
        nc = self.nc
        ready(nc.tensor)
        i, bank = self.slots.fill(nc.tensor, n)
        for c in range(KC):
            for t in range(T):
                last = nc.tensor.transpose(bank[:, (c * T + t) * P:(c * T + t + 1) * P],
                                           rows[:, t, c * P:(c + 1) * P], self.ident)
        self.slots.filled(i, last)
        self.slots.take(nc.scalar, n, i)
        copy = nc.scalar.copy(turned.rearrange("p c t q -> p (c t q)"), bank)
        return self.slots.taken(i, copy)

    def split(self, n, q, k):
        nc, dve, act, pool = self.nc, self.dve, self.act, self.pool
        src = [q.rearrange("p t (h d) -> p (t h) d", d=HD), k.rearrange("p t (h d) -> p (t h) d", d=HD)]
        rest = [self.rest[:, w].rearrange("p t (h d) -> p (t h) d", d=HD) for w in range(2)]
        dst = [x.rearrange("p t h r -> p (t h) r") for x in self.parts]
        order = (Q_PARTS, K_PARTS)

        def block(w, b):
            return dst[w][:, :, b * HD:(b + 1) * HD]

        step = [[0] * PARTS for _ in range(2)]
        for w in range(2):
            step[w][0] = act.done(nc.scalar.copy(block(w, order[w].index(0)), src[w]))
        for part in (1, 2):
            for w in range(2):
                act.wait(nc.vector, n, step[w][part - 1])
                last = order[w].index(part - 1)
                if part == 2:
                    out = block(w, order[w].index(2))
                    step[w][2] = dve.done(nc.vector.tensor_tensor(out, rest[w], block(w, last), ALU.subtract))
                else:
                    k_rest = dve.done(nc.vector.tensor_tensor(rest[w], src[w], block(w, last), ALU.subtract))
                    dve.wait(nc.scalar, n, k_rest)
                    step[w][1] = act.done(nc.scalar.copy(block(w, order[w].index(1)), rest[w]))
        for w in range(2):
            for part in (0, 1):
                act.hold(nc.gpsimd, n, step[w][part], self.idle_pool)
                first = order[w].index(part)
                for b in range(first + 1, 6):
                    if order[w][b] == part:
                        pool.done(nc.gpsimd.tensor_copy(block(w, b), block(w, first)))
        self.split_done = dve.k, pool.k
        yield

    def stacks(self, n):
        nc = self.nc
        self.dve.wait(nc.tensor, n, self.split_done[0])
        self.pool.wait(nc.tensor, n, self.split_done[1])
        for g in range(4):
            for w in range(2):
                i, bank = self.slots.fill(nc.tensor, n)
                turned = bank.bitcast(BF16)
                for j in range(4):
                    for t in range(T):
                        last = nc.tensor.transpose(turned[0:ROWS, (j * T + t) * P:(j * T + t + 1) * P],
                                                   self.parts[w][:, t, 4 * g + j, :], self.identb)
                self.slots.filled(i, last)
                engine = nc.scalar if w else nc.vector
                self.slots.take(engine, n, i)
                copy = nc.scalar.copy if w else nc.vector.tensor_copy
                out = self.stack[w][:, 4 * g:4 * g + 4].rearrange("r h t p -> r (h t p)")
                self.slots.taken(i, copy(out, turned[0:ROWS, :]))
                yield

    def maxima(self, n):
        nc, dve, v, pe = self.nc, self.dve, self.nc.vector, self.nc.tensor
        qs, ks = self.stack
        for s in self.slots.free:
            s.wait(pe, n)
        for h in range(H):
            i, bank = self.slots.fill(pe, n)
            for t in range(T):
                last = pe.matmul(bank[:, t * S:(t + 1) * S], qs[0:MAX0, h, t, :],
                                 ks[0:MAX0, h].rearrange("r t p -> r (t p)"), start=True, stop=True)
            self.slots.filled(i, last)
            self.slots.take(v, n, i)
            _, k = self.slots.taken(i, v.tensor_reduce(self.neg_max[:, :, h:h + 1],
                                                       bank.rearrange("p (t k) -> p t k", t=T),
                                                       AXX, ALU.max, negate=True))
            yield
        for s in self.slots.free:
            s.wait(v, n)
        mp = self.max_parts
        dve.done(v.tensor_copy(mp[:, :, 0, :], self.neg_max[:, :, :]))
        dve.wait(v, n)
        dve.done(v.tensor_tensor(self.max_rest[:, :, :], self.neg_max[:, :, :], mp[:, :, 0, :], ALU.subtract))
        dve.wait(v, n)
        dve.done(v.tensor_copy(mp[:, :, 1, :], self.max_rest[:, :, :]))
        dve.wait(v, n)
        k = dve.done(v.tensor_tensor(mp[:, :, 2, :], self.max_rest[:, :, :], mp[:, :, 1, :], ALU.subtract))
        yield
        dve.wait(pe, n, k)
        i, bank = self.slots.fill(pe, n)
        turned = bank.bitcast(BF16)
        for t in range(T):
            last = pe.transpose(turned[0:MAX_PARTS * H, t * P:(t + 1) * P],
                                mp[:, t].rearrange("p a h -> p (a h)"), self.identb)
        self.slots.filled(i, last)
        self.slots.take(v, n, i)
        free, k = self.slots.taken(i, v.tensor_copy(self.maxT[:, :, :].rearrange("r t p -> r (t p)"),
                                                    turned[0:PARTS * H, 0:S]))
        free.wait(nc.sync, n, k)
        for a in range(PARTS):
            self.max_dma.done(nc.sync.dma_start(qs[MAX0 + a:MAX0 + a + 1],
                                                self.maxT[a * H:(a + 1) * H, :, :]))
        yield

    def softmax_values(self, n, v_ready):
        nc, pe, act = self.nc, self.nc.tensor, self.nc.scalar
        qs, ks = self.stack
        exp_done = {}

        def scores(h):
            i, bank = self.slots.fill(pe, n)
            for t in range(T):
                last = pe.matmul(bank[:, t * S:(t + 1) * S], ks[:, h, t, :],
                                 qs[:, h].rearrange("r t p -> r (t p)"), start=True, stop=True)
            self.slots.filled(i, last)
            self.slots.take(act, n, i)
            if h >= 2:
                self.pv.wait(act, n, h - 1)
            exp_done[h] = self.slots.taken(i, act.activation(self.p[:, h % 2, :], bank, ACT.Exp,
                                                             scale=self.scale))

        def values(h):
            free, k = exp_done[h]
            free.wait(pe, n, k)
            g, j = h // 4, h % 4
            out = self.o_psum[32 * j:32 * j + 32, g // 2, (g % 2) * S:(g % 2 + 1) * S]
            for t in range(T):
                last = pe.matmul(out, self.v[:, t, h, :], self.p[:, h % 2, t * S:(t + 1) * S],
                                 start=(t == 0), stop=(t == T - 1))
            self.pv.done(last)

        self.max_dma.wait(pe, n)
        v_ready(pe)
        for h in range(H + 1):
            if h < H:
                scores(h)
            if h >= 1:
                values(h - 1)
            yield

    def outputs(self, n, weight):
        nc, pe, v, act, dve = self.nc, self.nc.tensor, self.nc.vector, self.nc.scalar, self.dve
        flat = self.oT[:, :, :].rearrange("p g s -> p (g s)")
        self.pv.wait(v, n)
        k_dve = dve.done(v.tensor_copy(flat[:, 0:BANK], self.o_psum[:, 0, :]))
        self.pv.wait(act, n)
        k_act = self.act.done(act.copy(flat[:, BANK:2 * BANK], self.o_psum[:, 1, :]))
        dve.wait(pe, n, k_dve)
        self.act.wait(pe, n, k_act)
        for t in range(T):
            i, bank = self.slots.fill(pe, n)
            for g in range(4):
                last = pe.transpose(bank[:, g * P:(g + 1) * P], self.oT[:, g, t * P:(t + 1) * P], self.ident)
            self.slots.filled(i, last)
            self.slots.take(v, n, i)
            heads = bank.rearrange("p (h w) -> p h w", w=VW)
            rden = self.rden[:, t, :].rearrange("p (h a) -> p h a", a=1)
            dve.done(v.reciprocal(rden, heads[:, :, HD:HD + 1]))
            dve.wait(v, n)
            ready, k = self.slots.taken(i, v.tensor_tensor(
                self.ctx[:, t, :].rearrange("p (h d) -> p h d", d=HD), heads[:, :, 0:HD],
                rden.broadcast_to([P, H, HD]), ALU.mult))
            yield

        def ctx_ready(engine):
            for s in self.slots.free:
                s.wait(engine, n)
        turned, k = self.turn_rows(n, self.ctx, self.ctxT[:, :, :, :], ctx_ready)
        turned.wait(pe, n, k)
        yield
        self.out_slot = self.project(n, self.ctxT, weight, D)

    def project(self, n, rowsT, weight, width):
        pe = self.nc.tensor
        i, bank = self.slots.fill(pe, n)
        for t in range(T):
            for c in range(KC):
                last = pe.matmul(bank[:, t * width:(t + 1) * width], rowsT[:, c, t, :], weight[:, c, :],
                                 start=(c == 0), stop=(c == KC - 1))
        self.slots.filled(i, last)
        return i, bank


def interleave(*passes):
    passes = list(passes)
    while passes:
        for p in list(passes):
            try:
                next(p)
            except StopIteration:
                passes.remove(p)


def rope_tables():
    position = np.arange(S)
    inv = np.float32(1.0) / np.float32(10000.0) ** (np.arange(2, dtype=np.float32) / np.float32(2.0))
    cos, sin = [], []
    for at in (position // 16, position % 16):
        freq = at.astype(np.float32)[:, None] * inv
        cos += [np.cos(freq), np.cos(freq)]
        s = np.concatenate([np.sin(freq), np.sin(freq)], axis=1)
        s[:, 0::2] *= -1
        sin.append(s)
    return np.concatenate(cos + sin, axis=1).astype(np.float32)


def build(nc, x, ctx_in, mask, wq, bq, wk, bk, wv, bv, wo, bo, w_fc, router_w, router_b, lang_w, lang_b,
          w1, b1, w2, b2, rope, out):
    v, act, pe, pool, sp = nc.vector, nc.scalar, nc.tensor, nc.gpsimd, nc.sync
    xg = nc.dram_tensor("rows_by_expert", [N_TILES * P, D], F32, kind="Internal").ap()
    yg = nc.dram_tensor("outs_by_expert", [N_TILES * P, D], F32, kind="Internal").ap()

    with ExitStack() as whole:
        def sb(name, shape, dt=F32, scope=whole):
            return scope.enter_context(nc.sbuf_tensor(name, shape, dt))

        def sem(name):
            return whole.enter_context(nc.semaphore(name))

        ident, identb = sb("ident", [P, P]), sb("identb", [P, P], BF16)
        upper, ones = sb("upper", [P, P]), sb("ones", [P, P])
        xs = sb("xs", [P, NT, D])
        rows = sb("rows", [P, NT, D])
        w1_sb = [sb("w1_sb0", [P, E, F])]
        logits = sb("logits", [P, NT, E + L])

        s_const, s_setup = Steps(sem("const"), 0), Steps(sem("setup"), 0)
        s_x0, s_x, s_ctx, s_small, s_w1, s_zero = (sem(f"load_{w}") for w in
                                                   ("x0", "x", "ctx", "small", "w1", "zero"))

        attention = ExitStack()
        wqkv = sb("wqkv", [P, KC, 3 * D], scope=attention)
        wo_sb = sb("wo_sb", [P, KC, D], scope=attention)
        fc_in = sb("fc_in", [P, KC, D], scope=attention)
        fc_sb = sb("fc_sb", [P, KC, D], scope=attention)
        r_in = sb("r_in", [E + L, D], scope=attention)
        r_sb = sb("r_sb", [P, KC, E + L], scope=attention)
        r_bias = sb("r_bias", [P, E + L], scope=attention)
        bias_qkv = sb("bias_qkv", [P, 3 * D], scope=attention)
        bias_o = sb("bias_o", [P, D], scope=attention)
        table = sb("table", [P, T, 2, 8], scope=attention)
        cx = sb("cx", [P, T, D], scope=attention)
        mask_in = sb("mask_in", [NT, P], I32, scope=attention)
        mask_f = sb("mask_f", [NT, P], scope=attention)
        keep = sb("keep", [P, NT], scope=attention)
        keep_n = sb("keep_n", [P, T], scope=attention)
        drop = sb("drop", [P, NT], scope=attention)
        neg = sb("neg", [P, NT, PARTS], BF16, scope=attention)
        qk = sb("qk", [P, 2, T, D], scope=attention)
        turn_a = sb("turn_a", [P, 2, T, H, 8], scope=attention)
        turn_b = sb("turn_b", [P, 2, T, H, 8], scope=attention)
        ctx_keep = sb("ctx_keep", [P, T, D], scope=attention)
        x_bias = sb("x_bias", [P, T, D], scope=attention)
        zeros = sb("zeros", [P, D], scope=attention)

        x_t = x.rearrange("b (t p) d -> p (b t) d", p=P)
        c_t = ctx_in.rearrange("b (t p) d -> p (b t) d", p=P)
        ctx_load = Steps(s_ctx, 1, by=16)
        sp.dma_start(xs[:, 0:T, :], x_t[:, 0:T, :]).then_inc(s_x0, 16)
        for i, w in enumerate((wq, wk, wv)):
            sp.dma_start(wqkv[:, :, i * D:(i + 1) * D], w.rearrange("(c p) n -> p c n", p=P)).then_inc(s_small, 16)
        small = 3
        for i, b_ in enumerate((bq, bk, bv)):
            sp.dma_start(bias_qkv[:, i * D:(i + 1) * D],
                         b_.rearrange("(a d) -> a d", a=1).broadcast_to([P, D])).then_inc(s_small, 16)
        sp.dma_start(table[:, :, :, :], rope.rearrange("(t p) (a d) -> p t a d", p=P, a=2)).then_inc(s_small, 16)
        sp.dma_start(bias_o[:, :], bo.rearrange("(a d) -> a d", a=1).broadcast_to([P, D])).then_inc(s_small, 16)
        sp.dma_start(r_bias[:, 0:E], router_b.rearrange("(a d) -> a d", a=1).broadcast_to([P, E])).then_inc(s_small, 16)
        sp.dma_start(r_bias[:, E:E + L], lang_b.rearrange("(a d) -> a d", a=1).broadcast_to([P, L])).then_inc(s_small, 16)
        sp.dma_start(wo_sb[:, :, :], wo.rearrange("(c p) n -> p c n", p=P)).then_inc(s_small, 16)
        sp.dma_start(fc_in[:, :, :], w_fc.rearrange("(c p) n -> p c n", p=P)).then_inc(s_small, 16)
        sp.dma_start(r_in[0:E, :], router_w).then_inc(s_small, 16)
        sp.dma_start(r_in[E:E + L, :], lang_w).then_inc(s_small, 16)
        sp.dma_start(mask_in[:, :], mask.rearrange("b a c (t p) -> (b a c t) p", p=P)).then_inc(s_small, 16)
        small += 3 + 9
        sp.dma_start(xs[:, T:NT, :], x_t[:, T:NT, :]).then_inc(s_x, 16)
        for e in range(E):
            sp.dma_start(w1_sb[0][:, e, :], w1[e, 0:P, :]).then_inc(s_w1, 16)

        s_const.done(pool.memset(ident[:, :], 0.0))
        s_const.done(pool.memset(upper[:, :], 1.0))
        s_const.wait(pool, 0)
        s_const.done(pool.affine_select(out=ident[:, :], in_=ident[:, :], compare_op=ALU.not_equal, fill=1.0,
                                        base=0, pattern=[[-1, P]], channel_multiplier=1))
        s_const.done(pool.affine_select(out=upper[:, :], in_=upper[:, :], compare_op=ALU.is_gt, fill=0.0,
                                        base=0, pattern=[[1, P]], channel_multiplier=-1))
        s_const.wait(pool, 0)
        s_const.done(pool.tensor_copy(identb[:, :], ident[:, :]))
        s_const.done(pool.memset(ones[:, :], 1.0))
        s_const.done(pool.memset(zeros[:, :], 0.0))

        steps_self = {"fills": 50, "dve": 39, "act": 5, "pool": 7}
        steps_cross = {"fills": 47, "dve": 53, "act": 5, "pool": 14}
        a1 = Attention(nc, attention, "self", ident[:, :], identb[:, :], HD ** -0.5, steps_self)
        a2 = Attention(nc, attention, "cross", ident[:, :], identb[:, :], 1.0 / D ** 0.5, steps_cross)
        for a in (a1, a2):
            a.slots.prime(nc)
            a.setup(s_const)

        s_const.wait(act, 0)
        for j in range(N_TILES):
            act.dma_start(xg[j * P:(j + 1) * P, :], zeros[:, :]).then_inc(s_zero, 16)

        bank = a2.psum[:, 3, :]
        s_const.wait(pe, 0)
        pe.wait_ge(s_small, 16 * small)
        for c in range(KC):
            for k in range(KC):
                last = pe.transpose(bank[:, (c * KC + k) * P:(c * KC + k + 1) * P], fc_in[:, k, c * P:(c + 1) * P], ident[:, :])
        s_setup.done(last)
        s_setup.wait(v, 0)
        s_setup.done(v.tensor_copy(fc_sb[:, :, :].rearrange("p c n -> p (c n)"), bank))
        v.wait_ge(s_small, 16 * small)
        s_setup.done(v.tensor_scalar(mask_f[:, :], mask_in[:, :], 0.0, None, ALU.not_equal))
        s_setup.wait(pe, 0)
        for c in range(KC):
            pe.transpose(bank[:, c * (E + L):(c + 1) * (E + L)], r_in[:, c * P:(c + 1) * P], ident[0:E + L, 0:E + L])
        s_setup.done(pe.transpose(bank[:, 2 * BANK // 4:2 * BANK // 4 + NT], mask_f[:, :], ident[0:NT, 0:NT]))
        s_setup.wait(v, 0)
        s_setup.done(v.tensor_copy(r_sb[:, :, :].rearrange("p c n -> p (c n)"), bank[:, 0:KC * (E + L)]))
        s_setup.done(v.tensor_copy(keep[:, :], bank[:, 2 * BANK // 4:2 * BANK // 4 + NT]))
        s_setup.wait(v, 0)
        s_setup.done(v.tensor_scalar(drop[:, :], keep[:, :], -1.0, 1.0, ALU.mult, ALU.add))
        s_setup.wait(v, 0)
        for a, part in enumerate(bf16_parts(NEG)):
            s_setup.done(v.tensor_scalar(neg[:, :, a], drop[:, :], part, None, ALU.mult))
        for engine in (v, act, pe, pool):
            s_setup.wait(engine, 0)
            s_const.wait(engine, 0)

        def residual(n):
            return xs[:, bass.ds(n * T, T), :]

        def self_pass(n):
            a = a1
            a.start()
            k = layer_norm(nc, n, a.dve, residual(n), a.xn[:, :, :], a.stats)
            yield
            turned, k_t = a.turn_rows(n, a.xn, a.xnT[:, :, :, :], lambda engine: a.dve.wait(engine, n, k))
            yield
            turned.wait(pe, n, k_t)
            for t in range(T):
                for lo, width in ((0, 2 * D), (2 * D, D)):
                    i, bank = a.slots.fill(pe, n)
                    for c in range(KC):
                        last = pe.matmul(bank[:, 0:width], a.xnT[:, c, t, :], wqkv[:, c, lo:lo + width],
                                         start=(c == 0), stop=(c == KC - 1))
                    a.slots.filled(i, last)
                    a.slots.take(v, n, i)
                    if lo == 0:
                        o = qk[:, :, t, :]
                        i0 = bank.rearrange("p (w d) -> p w d", w=2)
                        i1 = bias_qkv[:, 0:width].rearrange("p (w d) -> p w d", w=2)
                    else:
                        o = a.v[:, t, :, 0:HD]
                        i0 = bank[:, 0:D].rearrange("p (h d) -> p h d", d=HD)
                        i1 = bias_qkv[:, lo:lo + D].rearrange("p (h d) -> p h d", d=HD)
                    a.slots.taken(i, v.tensor_tensor(o, i0, i1, ALU.add))
                yield
            for s in a.slots.free:
                s.wait(v, n)
            v_step = [(s, s.k) for s in a.slots.free]
            part = qk[:, :, :, :].rearrange("p w t (h d) -> p w t h d", d=HD)[:, :, :, :, 4:12]
            for t in range(T):
                cos = table[:, t, 0, :].rearrange("p (a b d) -> p a b d", a=1, b=1).broadcast_to([P, 2, H, 8])
                a.dve.done(v.tensor_tensor(turn_a[:, :, t], part[:, :, t], cos, ALU.mult))
                for z in range(2):
                    sin = table[:, t, 1, :].rearrange("p (a b d) -> p a b d", a=1, b=1)[:, :, :, z::2]
                    a.dve.done(v.tensor_tensor(turn_b[:, :, t, :, z::2], part[:, :, t, :, 1 - z::2],
                                               sin.broadcast_to([P, 2, H, 4]), ALU.mult))
            a.dve.wait(v, n)
            k_rope = a.dve.done(v.tensor_tensor(part.rearrange("p w t h d -> p (w t h) d"),
                                                turn_a[:, :, :, :, :].rearrange("p w t h d -> p (w t h) d"),
                                                turn_b[:, :, :, :, :].rearrange("p w t h d -> p (w t h) d"), ALU.add))
            a.dve.wait(act, n, k_rope)
            a.dve.wait(v, n, k_rope)
            a.dve.wait(pool, n, k_rope)
            k_bias = a.pool.done(pool.tensor_tensor(x_bias[:, :, :], residual(n), bias_o[:, :]
                                                    .rearrange("p (a d) -> p a d", a=1).broadcast_to([P, T, D]), ALU.add))
            yield from a.split(n, qk[:, 0], qk[:, 1])
            yield from a.stacks(n)
            yield from a.maxima(n)
            yield from a.softmax_values(n, lambda engine: [s.wait(engine, n, k) for s, k in v_step])
            yield from a.outputs(n, wo_sb)
            i, bank = a.out_slot
            a.pool.wait(v, n, k_bias)
            a.slots.take(v, n, i)
            a.slots.taken(i, v.tensor_tensor(residual(n), bank.rearrange("p (t d) -> p t d", t=T),
                                             x_bias[:, :, :], ALU.add))
            yield
            a.end()

        def cross_pass(n):
            a = a2
            a.start()
            for s in a1.slots.free:
                s.wait(v, n, s.per_pass)
            k_norm = layer_norm(nc, n, a.dve, residual(n), a.xn[:, :, :], a.stats)
            a.dve.wait(sp, n, k_norm)
            ctx_load.start()
            ctx_load.done(sp.dma_start(cx[:, :, :], c_t[:, bass.ds(n * T, T), :]))
            a.dve.wait(pool, n, k_norm)
            a.pool.done(pool.tensor_copy(keep_n[:, :], keep[:, bass.ds(n * T, T)]))
            a.pool.wait(pool, n)
            ctx_load.hold(pool, n, idle=a.idle_pool)
            for t in range(T):
                a.pool.done(pool.tensor_scalar(ctx_keep[:, t, :], cx[:, t, :],
                                               keep_n[:, t:t + 1], None, ALU.mult))
            k_keys = a.pool.k
            for t in range(T):
                a.pool.done(pool.tensor_copy(a.v[:, t, :, 0:HD], cx[:, t, :].rearrange("p (h d) -> p h d", d=HD)))
                a.pool.done(pool.tensor_copy(a.parts[1][:, t, :, MASK0:MAX0],
                                             neg[:, bass.ds(n * T + t, 1), :].broadcast_to([P, H, PARTS])))
            k_values = a.pool.k
            yield
            a.dve.wait(act, n, k_norm)
            a.dve.wait(v, n, k_norm)
            a.pool.wait(act, n, k_keys)
            a.pool.wait(v, n, k_keys)
            yield from a.split(n, a.xn[:, :, :], ctx_keep[:, :, :])
            yield from a.stacks(n)
            yield from a.maxima(n)
            yield from a.softmax_values(n, lambda engine: a.pool.wait(engine, n, k_values))
            yield from a.outputs(n, fc_sb)
            i, bank = a.out_slot
            a.slots.take(v, n, i)
            free, k = a.slots.taken(i, v.tensor_tensor(residual(n), bank.rearrange("p (t d) -> p t d", t=T),
                                                       residual(n), ALU.add))
            free.wait(v, n, k)
            yield
            normed = rows[:, bass.ds(n * T, T), :]
            k = layer_norm(nc, n, a.dve, residual(n), a.xn[:, :, :], a.stats)
            a.dve.hold(pool, n, k, a.idle_pool)
            a.pool.done(pool.tensor_copy(normed, a.xn[:, :, :]))
            yield
            turned, k_t = a.turn_rows(n, a.xn, a.xnT[:, :, :, :], lambda engine: a.dve.wait(engine, n, k))
            yield
            turned.wait(pe, n, k_t)
            i, bank = a.project(n, a.xnT, r_sb, E + L)
            a.pool.wait(v, n)
            a.slots.take(v, n, i)
            a.slots.taken(i, v.tensor_tensor(
                logits[:, bass.ds(n * T, T), :], bank[:, 0:T * (E + L)].rearrange("p (t e) -> p t e", t=T),
                r_bias[:, :].rearrange("p (a e) -> p a e", a=1).broadcast_to([P, T, E + L]), ALU.add))
            yield
            a.end()

        v.wait_ge(s_x0, 16)
        interleave(self_pass(0))
        v.wait_ge(s_x, 16)
        pool.wait_ge(s_x, 16)
        with nc.Fori(1, B) as n:
            interleave(self_pass(n), cross_pass(n - 1))
        interleave(cross_pass(B - 1))

        for engine in (v, act, pe, pool, sp):
            for s in a2.slots.free:
                s.wait(engine, B - 1, s.per_pass)
            a2.pool.wait(engine, B - 1, a2.pool.per_pass)
        attention.close()
        return experts(nc, whole, sem, out, xs, rows, logits, ident, upper, ones, w1_sb, s_w1, s_zero,
                       w1, w2, b1, b2, xg, yg)


def route(nc, sb, sem, logits, upper, ones, bank):
    v, pe, pool, act = nc.vector, nc.tensor, nc.gpsimd, nc.scalar
    step = Steps(sem("route"), 0)

    def on(engine, instruction):
        step.done(instruction)
        step.wait(engine, 0)

    def tile(name, *shape, dt=F32):
        return sb(f"route_{name}", [P, *shape], dt)

    def last(ap, width):
        return ap.rearrange("p (t a) -> p t a", a=1).broadcast_to([P, NT, width])

    stat, recip = tile("stat", NT), tile("recip", NT)
    lang = tile("lang", NT, L + 1)
    z, prob = tile("z", NT, E), tile("prob", NT, E)
    hot = [tile(f"hot{i}", NT, E) for i in range(TOPK)]
    top = [tile(f"top{i}", NT) for i in range(TOPK)]
    gate = [tile(f"gate{i}", NT) for i in range(TOPK)]
    work, work2 = tile("work", NT, E), tile("work2", NT, E)
    order_i, order = tile("order_i", E, dt=I32), tile("order", E)
    index_i, index = tile("index_i", N_TILES, dt=I32), tile("index", N_TILES)
    dest = [tile(f"dest{i}", NT, dt=I32) for i in range(TOPK)]
    tile_expert = tile("tile_expert", N_TILES, dt=I32)

    on(pool, pool.iota(order_i[:, :], [[-1, E]], base=E, channel_multiplier=0))
    on(v, pool.iota(index_i[:, :], [[1, N_TILES]], base=0, channel_multiplier=0))
    on(v, v.tensor_copy(order[:, :], order_i[:, :]))
    on(v, v.tensor_copy(index[:, :], index_i[:, :]))

    def softmax(src, width, out):
        on(v, v.tensor_reduce(stat[:, :], src, AXX, ALU.max))
        on(act, v.tensor_tensor(out, src, last(stat[:, :], width), ALU.subtract))
        on(v, act.activation(out, out, ACT.Exp))
        on(v, v.tensor_reduce(stat[:, :], out, AXX, ALU.add))
        on(v, v.reciprocal(recip[:, :], stat[:, :]))
        on(v, v.tensor_tensor(out, out, last(recip[:, :], width), ALU.mult))

    on(v, v.memset(lang[:, :, L:L + 1], 0.0))
    softmax(logits[:, :, E:E + L], L, lang[:, :, 0:L])
    on(v, v.tensor_tensor(work[:, :, 0:L], lang[:, :, 0:L], lang[:, :, 1:L + 1], ALU.add))
    for i in range(E // L):
        on(v, v.scalar_tensor_tensor(out=z[:, :, i * L:(i + 1) * L], in0=work[:, :, 0:L], scalar=0.1,
                                     in1=logits[:, :, i * L:(i + 1) * L], op0=ALU.mult, op1=ALU.add))
    softmax(z[:, :, :], E, prob[:, :, :])

    order_all = order[:, :].rearrange("p (a e) -> p a e", a=1).broadcast_to([P, NT, E])
    for i in range(TOPK):
        on(v, v.tensor_reduce(top[i][:, :], prob[:, :, :], AXX, ALU.max))
        on(v, v.tensor_tensor(work[:, :, :], prob[:, :, :], last(top[i][:, :], E), ALU.is_equal))
        on(v, v.tensor_tensor(work[:, :, :], work[:, :, :], order_all, ALU.mult))
        on(v, v.tensor_reduce(stat[:, :], work[:, :, :], AXX, ALU.max))
        on(v, v.tensor_tensor(hot[i][:, :, :], work[:, :, :], last(stat[:, :], E), ALU.is_equal))
        if i == 0:
            on(v, v.scalar_tensor_tensor(out=prob[:, :, :], in0=hot[0][:, :, :], scalar=-2.0,
                                         in1=prob[:, :, :], op0=ALU.mult, op1=ALU.add))
    on(v, v.tensor_tensor(work2[:, :, :], hot[0][:, :, :], hot[1][:, :, :], ALU.add))
    step.wait(pe, 0)

    chosen = work2[:, :, :].rearrange("p t e -> p (t e)")
    before, total = bank[:, 0:NT * E], bank[:, NT * E:2 * NT * E]
    pe.matmul(before, upper[:, :], chosen, start=True, stop=True)
    on(v, pe.matmul(total, ones[:, :], chosen, start=True, stop=True))

    on(v, v.tensor_tensor(stat[:, :], top[0][:, :], top[1][:, :], ALU.add))
    on(v, v.reciprocal(recip[:, :], stat[:, :]))
    for i in range(TOPK):
        on(v, v.tensor_tensor(gate[i][:, :], top[i][:, :], recip[:, :], ALU.mult))

    sums = [prob, z]
    on(v, v.tensor_copy(work2[:, :, :].rearrange("p t e -> p (t e)"), total))
    on(v, v.tensor_copy(sums[0][:, :, :], work2[:, :, :]))
    for i, d in enumerate((1, 2, 4, 8)):
        a, b = sums[i % 2], sums[1 - i % 2]
        on(v, v.tensor_copy(b[:, 0:d, :], a[:, 0:d, :]))
        on(v, v.tensor_tensor(b[:, d:NT, :], a[:, d:NT, :], a[:, 0:NT - d, :], ALU.add))
    upto = sums[0]
    on(v, v.tensor_tensor(work2[:, :, :], upto[:, :, :], work2[:, :, :], ALU.subtract))

    fill_i, fill_i2 = tile("fill_i", E, dt=I32), tile("fill_i2", E, dt=I32)
    ends = [tile(f"ends{i}", E) for i in range(2)]
    tiles_of, start_row = tile("tiles_of", E), tile("start_row", E)
    on(v, v.tensor_scalar(fill_i[:, :], upto[:, NT - 1, :], float(P - 1), None, ALU.add))
    on(v, v.tensor_scalar(fill_i2[:, :], fill_i[:, :], P.bit_length() - 1, None, ALU.logical_shift_right))
    on(v, v.tensor_copy(tiles_of[:, :], fill_i2[:, :]))
    on(v, v.tensor_copy(ends[0][:, :], tiles_of[:, :]))
    for i, d in enumerate((1, 2, 4)):
        a, b = ends[i % 2], ends[1 - i % 2]
        on(v, v.tensor_copy(b[:, 0:d], a[:, 0:d]))
        on(v, v.tensor_tensor(b[:, d:E], a[:, d:E], a[:, 0:E - d], ALU.add))
    end = ends[1]
    on(v, v.tensor_tensor(start_row[:, :], end[:, :], tiles_of[:, :], ALU.subtract))
    on(v, v.tensor_scalar(start_row[:, :], start_row[:, :], float(P), None, ALU.mult))

    on(v, v.tensor_tensor(work2[:, :, :], work2[:, :, :], start_row[:, :]
                          .rearrange("p (a e) -> p a e", a=1).broadcast_to([P, NT, E]), ALU.add))
    on(v, v.tensor_tensor(work2[:, :, :].rearrange("p t e -> p (t e)"), before,
                          work2[:, :, :].rearrange("p t e -> p (t e)"), ALU.add))
    for i in range(TOPK):
        on(v, v.tensor_tensor(work[:, :, :], work2[:, :, :], hot[i][:, :, :], ALU.mult))
        on(v, v.tensor_reduce(stat[:, :], work[:, :, :], AXX, ALU.add))
        on(v, v.tensor_copy(dest[i][:, :], stat[:, :]))

    past = tile("past", N_TILES, E)
    on(v, v.tensor_tensor(past[:, :, :],
                          index[:, :].rearrange("p (j a) -> p j a", a=1).broadcast_to([P, N_TILES, E]),
                          end[:, :].rearrange("p (a e) -> p a e", a=1).broadcast_to([P, N_TILES, E]), ALU.is_ge))
    on(v, v.tensor_reduce(index[:, :], past[:, :, :], AXX, ALU.add))
    step.done(v.tensor_scalar(tile_expert[:, :], index[:, :], float(E - 1), None, ALU.min))
    return step, dest, gate, tile_expert


def experts(nc, whole, sem, out, xs, rows, logits, ident, upper, ones, w1_sb, s_w1, s_zero,
            w1, w2, b1, b2, xg, yg):
    v, act, pe, pool, sp = nc.vector, nc.scalar, nc.tensor, nc.gpsimd, nc.sync

    def sb(name, shape, dt=F32):
        return whole.enter_context(nc.sbuf_tensor(name, shape, dt))

    s_b, s_w1b, s_w2, s_b2 = (sem(f"load_{w}") for w in ("b1", "w1b", "w2", "b2"))
    w1_sb.append(sb("w1_sb1", [P, E, F]))
    w2_sb = sb("w2_sb", [P, E, FC, D])
    b1_in, b1_sb = sb("b1_in", [E * FC, P]), sb("b1_sb", [P, E, FC])
    b2_sb = sb("b2_sb", [P, E, D])
    sp.wait_ge(s_zero, 16 * N_TILES)
    sp.dma_start(b1_in[:, :], b1.rearrange("e (c p) -> (e c) p", p=P)).then_inc(s_b, 16)
    for e in range(E):
        sp.dma_start(w1_sb[1][:, e, :], w1[e, P:2 * P, :]).then_inc(s_w1b, 16)
    for e in range(E):
        sp.dma_start(b2_sb[:, e, :], b2[e:e + 1, :].broadcast_to([P, D])).then_inc(s_b2, 16)
        sp.dma_start(w2_sb[:, e, :, :], w2[e].rearrange("(c p) d -> p c d", p=P)).then_inc(s_w2, 16)

    psum = whole.enter_context(nc.psum_tensor("experts_psum", [P, 6, BANK], F32))
    h_bank, hT_bank = psum[:, 0:2, :].rearrange("p b n -> p (b n)"), psum[:, 2:4, :].rearrange("p b n -> p (b n)")
    x_bank, y_bank = psum[:, 4, :], psum[:, 5, :]

    s_bias = Steps(sem("bias"), 0)
    pe.wait_ge(s_b, 16)
    s_bias.done(pe.transpose(x_bank[:, 0:E * FC], b1_in[:, :], ident[0:E * FC, 0:E * FC]))
    s_bias.wait(v, 0)
    s_bias.done(v.tensor_copy(b1_sb[:, :, :].rearrange("p e c -> p (e c)"), x_bank[:, 0:E * FC]))

    step, dest, gate, tile_expert = route(nc, sb, sem, logits, upper, ones, y_bank)

    s_scatter = sem("scatter")
    step.wait(pool, 0)
    pool.wait_ge(s_zero, 16 * N_TILES)
    for t in range(NT):
        for i in range(TOPK):
            pool.indirect_dma_start(
                out=xg, out_offset=bass.IndirectOffsetOnAxis(ap=dest[i][:, t:t + 1].bitcast(U32), axis=0),
                in_=rows[:, t, :], in_offset=None).then_inc(s_scatter, 16)

    x_rows, xT = sb("x_rows", [P, D]), sb("xT", [P, KC, P])
    hid, hidT, y = sb("hid", [P, F]), sb("hidT", [P, FC, P]), sb("y", [P, D])
    load, turned_x, moved_x, up, moved_h, turned_h, gelu, down, moved_y, store = (
        Steps(sem(f"tile_{w}"), 1, by=by) for w, by in (
            ("load", 16), ("turned_x", 1), ("moved_x", 1), ("up", 1), ("moved_h", 1), ("turned_h", 1),
            ("gelu", 1), ("down", 1), ("moved_y", 1), ("store", 16)))

    def once(steps, instruction):
        steps.start()
        steps.done(instruction)

    def expert_of(engine, j):
        return engine.value_load(tile_expert[0:1, bass.ds(j, 1)], min_val=0, max_val=E - 1)

    def load_x(j, first=False):
        if not first:
            turned_x.wait(sp, j - 1, 1)
        once(load, sp.dma_start(x_rows[:, :], xg[bass.ds(j * P, P), :]))

    def turn_x(j):
        load.wait(pe, j, 1)
        for c in range(KC):
            last = pe.transpose(x_bank[:, c * P:(c + 1) * P], x_rows[:, c * P:(c + 1) * P], ident[:, :])
        once(turned_x, last)
        turned_x.wait(v, j, 1)
        once(moved_x, v.tensor_copy(xT[:, :, :].rearrange("p c t -> p (c t)"), x_bank[:, 0:D]))

    def up_layer(j):
        moved_x.wait(pe, j, 1)
        e = expert_of(pe, j)
        for half in range(F // BANK):
            for c in range(KC):
                last = pe.matmul(h_bank[:, half * BANK:(half + 1) * BANK], xT[:, c, :],
                                 w1_sb[c][:, bass.ds(e, 1), half * BANK:(half + 1) * BANK]
                                 .rearrange("p a n -> p (a n)"), start=(c == 0), stop=(c == KC - 1))
        once(up, last)
        up.wait(v, j, 1)
        once(moved_h, v.tensor_copy(hid[:, :], h_bank))

    def turn_h(j):
        moved_h.wait(pe, j, 1)
        for c in range(FC):
            last = pe.transpose(hT_bank[:, c * P:(c + 1) * P], hid[:, c * P:(c + 1) * P], ident[:, :])
        once(turned_h, last)
        e = expert_of(act, j)
        turned_h.wait(act, j, 1)
        for c in range(FC):
            last = act.activation(hidT[:, c, :], hT_bank[:, c * P:(c + 1) * P], ACT.Gelu,
                                  bias=b1_sb[:, bass.ds(e, 1), c])
        once(gelu, last)

    def down_layer(j, first=False):
        e = expert_of(pe, j)
        gelu.wait(pe, j, 1)
        if not first:
            moved_y.wait(pe, j - 1, 1)
        for c in range(FC):
            last = pe.matmul(y_bank[:, 0:D], hidT[:, c, :],
                             w2_sb[:, bass.ds(e, 1), c, :].rearrange("p a n -> p (a n)"),
                             start=(c == 0), stop=(c == FC - 1))
        once(down, last)
        e = expert_of(v, j)
        if not first:
            store.wait(v, j - 1, 1)
        down.wait(v, j, 1)
        once(moved_y, v.tensor_tensor(y[:, :], y_bank[:, 0:D],
                                      b2_sb[:, bass.ds(e, 1), :].rearrange("p a n -> p (a n)"), ALU.add))
        moved_y.wait(sp, j, 1)
        once(store, sp.dma_start(yg[bass.ds(j * P, P), :], y[:, :]))

    sp.wait_ge(s_scatter, 16 * NT * TOPK)
    for engine in (v, act, pe):
        step.wait(engine, 0)
        s_bias.wait(engine, 0)
    pe.wait_ge(s_w1, 16 * E)
    pe.wait_ge(s_w1b, 16 * E)
    load_x(0, first=True)
    turn_x(0)
    up_layer(0)
    load_x(1)
    turn_x(1)
    load_x(2)
    turn_h(0)
    up_layer(1)
    turn_x(2)
    pe.wait_ge(s_w2, 16 * E)
    v.wait_ge(s_b2, 16 * E)
    down_layer(0, first=True)
    with nc.Fori(1, N_TILES - 2) as j:
        load_x(j + 2)
        turn_h(j)
        up_layer(j + 1)
        turn_x(j + 2)
        down_layer(j)
    turn_h(N_TILES - 2)
    up_layer(N_TILES - 1)
    down_layer(N_TILES - 2)
    turn_h(N_TILES - 1)
    down_layer(N_TILES - 1)

    s_gather = [sem(f"gather{i}") for i in range(TOPK)]
    s_sum, s_out = Steps(sem("sum"), 0), sem("out")
    got = [rows, sb("got", [P, NT, D])]
    store.wait(pool, N_TILES - 1, 1)
    out_t = out.rearrange("b (t p) d -> p (b t) d", p=P)
    for t in range(NT):
        for i in range(TOPK):
            pool.indirect_dma_start(
                out=got[i][:, t, :], out_offset=None, in_=yg,
                in_offset=bass.IndirectOffsetOnAxis(ap=dest[i][:, t:t + 1].bitcast(U32), axis=0)
            ).then_inc(s_gather[i], 16)
    for i in range(TOPK):
        v.wait_ge(s_gather[i], 16 * NT)
    for t in range(NT):
        for i in range(TOPK):
            s_sum.wait(v, 0)
            s_sum.done(v.scalar_tensor_tensor(out=xs[:, t, :], in0=got[i][:, t, :], scalar=gate[i][:, t:t + 1],
                                              in1=xs[:, t, :], op0=ALU.mult, op1=ALU.add))
        s_sum.wait(sp, 0)
        sp.dma_start(out_t[:, t, :], xs[:, t, :]).then_inc(s_out, 16)
    sp.wait_ge(s_out, 16 * NT)


_INS = ["x", "ctx_1024", "mask_Bx1x1xS2_ik0", "L0_attn_Wq", "L0_attn_bq", "L0_attn_Wk", "L0_attn_bk",
        "L0_attn_Wv", "L0_attn_bv", "L0_attn_Wo", "L0_attn_bo", "L0_xattn_W_fc", "L0_ffn_router_w",
        "L0_ffn_router_b", "L0_ffn_lang_w", "L0_ffn_lang_b", "L0_ffn_w1", "L0_ffn_b1", "L0_ffn_w2",
        "L0_ffn_b2"]


def kernel(**inputs):
    import concourse.bacc as bacc
    from concourse.bass_utils import run_bass_kernel_spmd

    nc = bacc.Bacc("TRN2", target_bir_lowering=False, num_devices=1)
    arrays = {f"in_{name}": np.ascontiguousarray(inputs[name]) for name in _INS}
    arrays["rope"] = rope_tables()
    args = [nc.dram_tensor(name, a.shape, mybir.dt.from_np(a.dtype), kind="ExternalInput").ap()
            for name, a in arrays.items()]
    out = nc.dram_tensor("out", (B, S, D), F32, kind="ExternalOutput").ap()
    build(nc, *args, out)
    r = run_bass_kernel_spmd(nc, [arrays], core_ids=[0])
    return r.results[0]["out"]
```

```python
from contextlib import ExitStack
from itertools import chain

import numpy as np

import concourse.bass as bass
from concourse import mybir

F32 = mybir.dt.float32
BF16 = mybir.dt.bfloat16
I32 = mybir.dt.int32
U32 = mybir.dt.uint32
ALU = mybir.AluOpType
ACT = mybir.ActivationFunctionType
AXX = mybir.AxisListType.X

P = 128
B, S, D = 8, 256, 256
H, HD = 16, 16
T = S // P
KC = D // P
NT = B * T
PARTS = 3
Q_PARTS = (0, 0, 0, 1, 1, 2)
K_PARTS = (0, 1, 2, 0, 1, 0)
STACK = 6 * HD
MASK0 = STACK
MAX0 = STACK + PARTS
ROWS = STACK + 2 * PARTS
VW = 32
BANK = 512
MAX_PARTS = 5
NEG = -1e20
EPS = 1e-5
E, L, TOPK, F = 8, 4, 2, 1024
FC = F // P
N_TILES = (NT * P * TOPK - E) // P + E
RSQRT_MAGIC = 0x5F3759DF


def bf16_parts(value):
    rest, out = np.array([value], np.float32), []
    for _ in range(PARTS):
        part = (rest.view(np.uint32) & np.uint32(0xFFFF0000)).view(np.float32)
        out.append(float(part[0]))
        rest = rest - part
    return out


class Steps:

    def __init__(self, sem, per_pass, credit=0, by=1):
        self.sem, self.per_pass, self.credit, self.by, self.k = sem, per_pass, credit, by, 0

    def start(self):
        self.k = 0

    def end(self):
        assert self.k == self.per_pass, (self.sem.name, self.k, self.per_pass)

    def done(self, instruction):
        self.k += 1
        instruction.then_inc(self.sem, self.by)
        return self.k

    def wait(self, engine, n, k=None):
        k = self.k if k is None else k
        engine.wait_ge(self.sem, (n * self.per_pass + k) * self.by + self.credit)

    def hold(self, engine, n, k=None, idle=None):
        self.wait(engine, n, k)
        engine.sem_inc(idle, 1)


class Slots:

    def __init__(self, full, free, banks, fills_per_pass):
        per_pass = [(fills_per_pass + 1) // 2, fills_per_pass // 2]
        self.full = [Steps(s, k) for s, k in zip(full, per_pass)]
        self.free = [Steps(s, k, credit=1) for s, k in zip(free, per_pass)]
        self.banks, self.unit = banks, 0

    def prime(self, nc):
        for s in self.free:
            nc.vector.sem_inc(s.sem, 1)

    def start(self):
        self.unit = 0
        for s in self.full + self.free:
            s.start()

    def end(self):
        for s in self.full + self.free:
            s.end()

    def fill(self, pe, n):
        i = self.unit % 2
        self.unit += 1
        self.free[i].wait(pe, n)
        return i, self.banks[i]

    def filled(self, i, instruction):
        self.full[i].done(instruction)

    def take(self, engine, n, i):
        self.full[i].wait(engine, n)

    def taken(self, i, instruction):
        return self.free[i], self.free[i].done(instruction)


def layer_norm(nc, n, dve, src, dst, st):
    v = nc.vector
    for t in range(T):
        dve.done(v.bn_stats(st["bn"][:, t, :], src[:, t, :]))
    dve.hold(v, n, idle=st["idle"])
    for t in range(T):
        dve.done(v.bn_aggr(st["mv"][:, t, :], st["bn"][:, t, :]))
    dve.wait(v, n)
    var, y, w = st["var"][:, :], st["rstd"][:, :], st["tmp"][:, :]
    dve.done(v.tensor_scalar(var, st["mv"][:, :, 1], EPS, None, ALU.add))
    dve.wait(v, n)
    dve.done(v.tensor_scalar(w.bitcast(I32), var.bitcast(I32), 1, None, ALU.logical_shift_right))
    dve.wait(v, n)
    dve.done(v.tensor_scalar(y.bitcast(I32), w.bitcast(I32), -1, float(RSQRT_MAGIC), ALU.mult, ALU.add))
    for _ in range(3):
        dve.wait(v, n)
        dve.done(v.tensor_tensor(w, y, y, ALU.mult))
        dve.wait(v, n)
        dve.done(v.scalar_tensor_tensor(out=w, in0=w, scalar=-0.5, in1=var, op0=ALU.mult, op1=ALU.mult))
        dve.wait(v, n)
        dve.done(v.scalar_tensor_tensor(out=y, in0=w, scalar=1.5, in1=y, op0=ALU.add, op1=ALU.mult))
    dve.wait(v, n)
    for t in range(T):
        k = dve.done(v.tensor_scalar(dst[:, t, :], src[:, t, :], st["mv"][:, t, 0:1], y[:, t:t + 1],
                                     ALU.subtract, ALU.mult))
    return k


class Attention:

    def __init__(self, nc, ctx, name, ident, identb, scale, steps):
        self.nc, self.name, self.scale, self.ident, self.identb = nc, name, scale, ident, identb

        def sb(what, shape, dt=F32):
            return ctx.enter_context(nc.sbuf_tensor(f"{name}_{what}", shape, dt))

        def sem(what):
            return ctx.enter_context(nc.semaphore(f"{name}_{what}"))

        self.psum = ctx.enter_context(nc.psum_tensor(f"{name}_psum", [P, 4, BANK], F32))
        self.slots = Slots([sem("full0"), sem("full1")], [sem("free0"), sem("free1")],
                           [self.psum[:, 0, :], self.psum[:, 1, :]], steps["fills"])
        self.o_psum = self.psum[:, 2:4, :]
        self.dve = Steps(sem("dve"), steps["dve"])
        self.act = Steps(sem("act"), steps["act"])
        self.pool = Steps(sem("pool"), steps["pool"])
        self.pv = Steps(sem("pv"), H)
        self.max_dma = Steps(sem("max_dma"), PARTS, by=16)
        self.all = [self.slots, self.dve, self.act, self.pool, self.pv, self.max_dma]

        self.stats = {"bn": sb("bn", [P, T, 6]), "mv": sb("mv", [P, T, 2]), "var": sb("var", [P, T]),
                      "rstd": sb("rstd", [P, T]), "tmp": sb("tmp", [P, T]), "idle": sem("idle_dve")}
        self.idle_pool = sem("idle_pool")
        self.xn = sb("xn", [P, T, D])
        self.xnT = sb("xnT", [P, KC, T, P])
        self.rest = sb("rest", [P, 2, T, D])
        self.parts = [sb(f"parts_{w}", [P, T, H, ROWS], BF16) for w in "qk"]
        self.stack = [sb(f"stack_{w}", [ROWS, H, T, P], BF16) for w in "qk"]
        self.v = sb("v", [P, T, H, VW])
        self.neg_max = sb("neg_max", [P, T, H])
        self.max_rest = sb("max_rest", [P, T, H])
        self.max_parts = sb("max_parts", [P, T, MAX_PARTS, H], BF16)
        self.maxT = sb("maxT", [PARTS * H, T, P], BF16)
        self.p = sb("p", [P, 2, BANK])
        self.oT = self.rest[:, :, :, :].rearrange("p w t d -> p (w t) d")
        self.rden = sb("rden", [P, T, H])
        self.ctx, self.ctxT = self.xn, self.xnT

    def setup(self, count):
        nc = self.nc
        q, k = self.parts
        count.done(nc.gpsimd.memset(self.max_parts[:, :, :, :], 0.0))
        for what, value in ((q[:, :, :, MASK0:MAX0], 1.0), (q[:, :, :, MAX0:ROWS], 0.0),
                            (k[:, :, :, MASK0:MAX0], 0.0), (k[:, :, :, MAX0:ROWS], 1.0),
                            (self.v[:, :, :, HD:HD + 1], 1.0), (self.v[:, :, :, HD + 1:VW], 0.0)):
            count.done(nc.gpsimd.memset(what, value))

    def start(self):
        for s in self.all:
            s.start()

    def end(self):
        for s in self.all:
            s.end()

    def turn_rows(self, n, rows, turned, ready):
        nc = self.nc
        ready(nc.tensor)
        i, bank = self.slots.fill(nc.tensor, n)
        for c in range(KC):
            for t in range(T):
                last = nc.tensor.transpose(bank[:, (c * T + t) * P:(c * T + t + 1) * P],
                                           rows[:, t, c * P:(c + 1) * P], self.ident)
        self.slots.filled(i, last)
        self.slots.take(nc.scalar, n, i)
        copy = nc.scalar.copy(turned.rearrange("p c t q -> p (c t q)"), bank)
        return self.slots.taken(i, copy)

    def split(self, n, q, k):
        nc, dve, act = self.nc, self.dve, self.act
        src = [q.rearrange("p t (h d) -> p (t h) d", d=HD), k.rearrange("p t (h d) -> p (t h) d", d=HD)]
        rest = [self.rest[:, w].rearrange("p t (h d) -> p (t h) d", d=HD) for w in range(2)]
        dst = [x.rearrange("p t h r -> p (t h) r") for x in self.parts]
        order = (Q_PARTS, K_PARTS)

        def block(w, b):
            return dst[w][:, :, b * HD:(b + 1) * HD]

        def again(w, part):
            at = [b for b in range(6) if order[w][b] == part]
            blocks = dst[w][:, :, 0:STACK].rearrange("p g (b d) -> p g b d", d=HD)
            dve.done(nc.vector.tensor_copy(
                blocks[:, :, at[1]:at[-1] + 1:at[-1] - at[-2], :],
                blocks[:, :, at[0]:at[0] + 1, :].broadcast_to([P, T * H, len(at) - 1, HD])))

        def rounded(w, part, src):
            return act.done(nc.scalar.copy(block(w, order[w].index(part)), src))

        k_part = [rounded(w, 0, src[w]) for w in range(2)]
        yield 0.8
        for w in range(2):
            act.wait(nc.vector, n, k_part[w])
            k_rest = dve.done(nc.vector.tensor_tensor(rest[w], src[w], block(w, order[w].index(0)), ALU.subtract))
            dve.wait(nc.scalar, n, k_rest)
            k_part[w] = rounded(w, 1, rest[w])
        yield 1.2
        for w in range(2):
            again(w, 0)
        yield 1.5
        for w in range(2):
            act.wait(nc.vector, n, k_part[w])
            dve.done(nc.vector.tensor_tensor(block(w, order[w].index(2)), rest[w],
                                             block(w, order[w].index(1)), ALU.subtract))
        yield 1.2
        for w in range(2):
            again(w, 1)
        self.split_done = dve.k
        yield 1.0

    def stacks(self, n):
        nc = self.nc
        self.dve.wait(nc.tensor, n, self.split_done)
        for g in range(4):
            for w in range(2):
                i, bank = self.slots.fill(nc.tensor, n)
                turned = bank.bitcast(BF16)
                for j in range(4):
                    for t in range(T):
                        last = nc.tensor.transpose(turned[0:ROWS, (j * T + t) * P:(j * T + t + 1) * P],
                                                   self.parts[w][:, t, 4 * g + j, :], self.identb)
                self.slots.filled(i, last)
                engine = nc.scalar if w else nc.vector
                self.slots.take(engine, n, i)
                copy = nc.scalar.copy if w else nc.vector.tensor_copy
                out = self.stack[w][:, 4 * g:4 * g + 4].rearrange("r h t p -> r (h t p)")
                self.slots.taken(i, copy(out, turned[0:ROWS, :]))
                yield 0.7

    def maxima(self, n):
        nc, dve, v, pe = self.nc, self.dve, self.nc.vector, self.nc.tensor
        qs, ks = self.stack
        for s in self.slots.free:
            s.wait(pe, n)
        for h in range(H):
            i, bank = self.slots.fill(pe, n)
            for t in range(T):
                last = pe.matmul(bank[:, t * S:(t + 1) * S], qs[0:MAX0, h, t, :],
                                 ks[0:MAX0, h].rearrange("r t p -> r (t p)"), start=True, stop=True)
            self.slots.filled(i, last)
            self.slots.take(v, n, i)
            _, k = self.slots.taken(i, v.tensor_reduce(self.neg_max[:, :, h:h + 1],
                                                       bank.rearrange("p (t k) -> p t k", t=T),
                                                       AXX, ALU.max, negate=True))
            yield 0.65
        for s in self.slots.free:
            s.wait(v, n)
        mp = self.max_parts
        dve.done(v.tensor_copy(mp[:, :, 0, :], self.neg_max[:, :, :]))
        dve.wait(v, n)
        dve.done(v.tensor_tensor(self.max_rest[:, :, :], self.neg_max[:, :, :], mp[:, :, 0, :], ALU.subtract))
        dve.wait(v, n)
        dve.done(v.tensor_copy(mp[:, :, 1, :], self.max_rest[:, :, :]))
        dve.wait(v, n)
        k = dve.done(v.tensor_tensor(mp[:, :, 2, :], self.max_rest[:, :, :], mp[:, :, 1, :], ALU.subtract))
        yield 1.2
        dve.wait(pe, n, k)
        i, bank = self.slots.fill(pe, n)
        turned = bank.bitcast(BF16)
        for t in range(T):
            last = pe.transpose(turned[0:MAX_PARTS * H, t * P:(t + 1) * P],
                                mp[:, t].rearrange("p a h -> p (a h)"), self.identb)
        self.slots.filled(i, last)
        self.slots.take(v, n, i)
        free, k = self.slots.taken(i, v.tensor_copy(self.maxT[:, :, :].rearrange("r t p -> r (t p)"),
                                                    turned[0:PARTS * H, 0:S]))
        free.wait(nc.sync, n, k)
        for a in range(PARTS):
            self.max_dma.done(nc.sync.dma_start(qs[MAX0 + a:MAX0 + a + 1],
                                                self.maxT[a * H:(a + 1) * H, :, :]))
        yield 4.0

    def softmax_values(self, n, v_ready):
        nc, pe, act = self.nc, self.nc.tensor, self.nc.scalar
        qs, ks = self.stack
        exp_done = {}

        def scores(h):
            i, bank = self.slots.fill(pe, n)
            for t in range(T):
                last = pe.matmul(bank[:, t * S:(t + 1) * S], ks[:, h, t, :],
                                 qs[:, h].rearrange("r t p -> r (t p)"), start=True, stop=True)
            self.slots.filled(i, last)
            self.slots.take(act, n, i)
            if h >= 2:
                self.pv.wait(act, n, h - 1)
            exp_done[h] = self.slots.taken(i, act.activation(self.p[:, h % 2, :], bank, ACT.Exp,
                                                             scale=self.scale))

        def values(h):
            free, k = exp_done[h]
            free.wait(pe, n, k)
            g, j = h // 4, h % 4
            out = self.o_psum[32 * j:32 * j + 32, g // 2, (g % 2) * S:(g % 2 + 1) * S]
            for t in range(T):
                last = pe.matmul(out, self.v[:, t, h, :], self.p[:, h % 2, t * S:(t + 1) * S],
                                 start=(t == 0), stop=(t == T - 1))
            self.pv.done(last)

        self.max_dma.wait(pe, n)
        v_ready(pe)
        for h in range(H + 1):
            if h < H:
                scores(h)
            if h >= 1:
                values(h - 1)
            yield 1.1

    def outputs(self, n, weight):
        nc, pe, v, act, dve = self.nc, self.nc.tensor, self.nc.vector, self.nc.scalar, self.dve
        flat = self.oT[:, :, :].rearrange("p g s -> p (g s)")
        self.pv.wait(v, n)
        k_dve = dve.done(v.tensor_copy(flat[:, 0:BANK], self.o_psum[:, 0, :]))
        self.pv.wait(act, n)
        k_act = self.act.done(act.copy(flat[:, BANK:2 * BANK], self.o_psum[:, 1, :]))
        dve.wait(pe, n, k_dve)
        yield 1.2
        self.act.wait(pe, n, k_act)
        for t in range(T):
            i, bank = self.slots.fill(pe, n)
            for g in range(4):
                last = pe.transpose(bank[:, g * P:(g + 1) * P], self.oT[:, g, t * P:(t + 1) * P], self.ident)
            self.slots.filled(i, last)
            self.slots.take(v, n, i)
            heads = bank.rearrange("p (h w) -> p h w", w=VW)
            rden = self.rden[:, t, :].rearrange("p (h a) -> p h a", a=1)
            dve.done(v.reciprocal(rden, heads[:, :, HD:HD + 1]))
            dve.wait(v, n)
            ready, k = self.slots.taken(i, v.tensor_tensor(
                self.ctx[:, t, :].rearrange("p (h d) -> p h d", d=HD), heads[:, :, 0:HD],
                rden.broadcast_to([P, H, HD]), ALU.mult))
            yield 1.2

        def ctx_ready(engine):
            for s in self.slots.free:
                s.wait(engine, n)
        turned, k = self.turn_rows(n, self.ctx, self.ctxT[:, :, :, :], ctx_ready)
        yield 1.3
        turned.wait(pe, n, k)
        self.out_slot = self.project(n, self.ctxT, weight, D)

    def project(self, n, rowsT, weight, width):
        pe = self.nc.tensor
        i, bank = self.slots.fill(pe, n)
        for t in range(T):
            for c in range(KC):
                last = pe.matmul(bank[:, t * width:(t + 1) * width], rowsT[:, c, t, :], weight[:, c, :],
                                 start=(c == 0), stop=(c == KC - 1))
        self.slots.filled(i, last)
        return i, bank


def interleave(*passes):
    at = [0.0] * len(passes)
    while min(at) < float("inf"):
        i = at.index(min(at))
        at[i] += next(passes[i], float("inf"))


def rope_tables():
    position = np.arange(S)
    inv = np.float32(1.0) / np.float32(10000.0) ** (np.arange(2, dtype=np.float32) / np.float32(2.0))
    cos, sin = [], []
    for at in (position // 16, position % 16):
        freq = at.astype(np.float32)[:, None] * inv
        cos += [np.cos(freq), np.cos(freq)]
        s = np.concatenate([np.sin(freq), np.sin(freq)], axis=1)
        s[:, 0::2] *= -1
        sin.append(s)
    return np.concatenate(cos + sin, axis=1).astype(np.float32)


def build(nc, x, ctx_in, mask, wq, bq, wk, bk, wv, bv, wo, bo, w_fc, router_w, router_b, lang_w, lang_b,
          w1, b1, w2, b2, rope, out):
    v, act, pe, pool, sp = nc.vector, nc.scalar, nc.tensor, nc.gpsimd, nc.sync
    rows = nc.dram_tensor("rows", [NT * P + P, D], F32, kind="Internal").ap()

    with ExitStack() as whole:
        def sb(name, shape, dt=F32, scope=whole):
            return scope.enter_context(nc.sbuf_tensor(name, shape, dt))

        def sem(name):
            return whole.enter_context(nc.semaphore(name))

        ident, identb = sb("ident", [P, P]), sb("identb", [P, P], BF16)
        upper, ones = sb("upper", [P, P]), sb("ones", [P, P])
        xs = sb("xs", [P, NT, D])
        w1_sb = [sb("w1_sb0", [P, E, F])]
        logits = sb("logits", [P, NT, E + L])

        s_const, s_setup = Steps(sem("const"), 0), Steps(sem("setup"), 0)
        s_x0, s_x, s_ctx, s_small, s_w1, s_zero = (sem(f"load_{w}") for w in
                                                   ("x0", "x", "ctx", "small", "w1", "zero"))
        stored = Steps(sem("stored"), 2, by=16)

        attention = ExitStack()
        wqkv = sb("wqkv", [P, KC, 3 * D], scope=attention)
        wo_sb = sb("wo_sb", [P, KC, D], scope=attention)
        fc_in = sb("fc_in", [P, KC, D], scope=attention)
        fc_sb = sb("fc_sb", [P, KC, D], scope=attention)
        r_in = sb("r_in", [E + L, D], scope=attention)
        r_sb = sb("r_sb", [P, KC, E + L], scope=attention)
        r_bias = sb("r_bias", [P, E + L], scope=attention)
        bias_qkv = sb("bias_qkv", [P, 3 * D], scope=attention)
        bias_o = sb("bias_o", [P, D], scope=attention)
        table = sb("table", [P, T, 2, 8], scope=attention)
        cx = sb("cx", [P, T, D], scope=attention)
        mask_in = sb("mask_in", [NT, P], I32, scope=attention)
        mask_f = sb("mask_f", [NT, P], scope=attention)
        keep = sb("keep", [P, NT], scope=attention)
        keep_n = sb("keep_n", [P, T], scope=attention)
        drop = sb("drop", [P, NT], scope=attention)
        neg = sb("neg", [P, NT, PARTS], BF16, scope=attention)
        qk = sb("qk", [P, 2, T, D], scope=attention)
        turn_a = sb("turn_a", [P, 2, T, H, 8], scope=attention)
        turn_b = sb("turn_b", [P, 2, T, H, 8], scope=attention)
        ctx_keep = sb("ctx_keep", [P, T, D], scope=attention)
        x_bias = sb("x_bias", [P, T, D], scope=attention)
        zeros = sb("zeros", [P, D], scope=attention)

        x_t = x.rearrange("b (t p) d -> p (b t) d", p=P)
        out_t = out[0:NT * P, :].rearrange("(t p) d -> p t d", p=P)
        rows_t = rows[0:NT * P, :].rearrange("(t p) d -> p t d", p=P)
        c_t = ctx_in.rearrange("b (t p) d -> p (b t) d", p=P)
        ctx_load = Steps(s_ctx, 1, by=16)
        sp.dma_start(xs[:, 0:T, :], x_t[:, 0:T, :]).then_inc(s_x0, 16)
        for i, w in enumerate((wq, wk, wv)):
            sp.dma_start(wqkv[:, :, i * D:(i + 1) * D], w.rearrange("(c p) n -> p c n", p=P)).then_inc(s_small, 16)
        small = 3
        for i, b_ in enumerate((bq, bk, bv)):
            sp.dma_start(bias_qkv[:, i * D:(i + 1) * D],
                         b_.rearrange("(a d) -> a d", a=1).broadcast_to([P, D])).then_inc(s_small, 16)
        sp.dma_start(table[:, :, :, :], rope.rearrange("(t p) (a d) -> p t a d", p=P, a=2)).then_inc(s_small, 16)
        sp.dma_start(bias_o[:, :], bo.rearrange("(a d) -> a d", a=1).broadcast_to([P, D])).then_inc(s_small, 16)
        sp.dma_start(r_bias[:, 0:E], router_b.rearrange("(a d) -> a d", a=1).broadcast_to([P, E])).then_inc(s_small, 16)
        sp.dma_start(r_bias[:, E:E + L], lang_b.rearrange("(a d) -> a d", a=1).broadcast_to([P, L])).then_inc(s_small, 16)
        sp.dma_start(wo_sb[:, :, :], wo.rearrange("(c p) n -> p c n", p=P)).then_inc(s_small, 16)
        sp.dma_start(fc_in[:, :, :], w_fc.rearrange("(c p) n -> p c n", p=P)).then_inc(s_small, 16)
        sp.dma_start(r_in[0:E, :], router_w).then_inc(s_small, 16)
        sp.dma_start(r_in[E:E + L, :], lang_w).then_inc(s_small, 16)
        sp.dma_start(mask_in[:, :], mask.rearrange("b a c (t p) -> (b a c t) p", p=P)).then_inc(s_small, 16)
        small += 3 + 9
        sp.dma_start(xs[:, T:NT, :], x_t[:, T:NT, :]).then_inc(s_x, 16)
        for e in range(E):
            sp.dma_start(w1_sb[0][:, e, :], w1[e, 0:P, :]).then_inc(s_w1, 16)

        s_const.done(pool.memset(ident[:, :], 0.0))
        s_const.done(pool.memset(upper[:, :], 1.0))
        s_const.wait(pool, 0)
        s_const.done(pool.affine_select(out=ident[:, :], in_=ident[:, :], compare_op=ALU.not_equal, fill=1.0,
                                        base=0, pattern=[[-1, P]], channel_multiplier=1))
        s_const.done(pool.affine_select(out=upper[:, :], in_=upper[:, :], compare_op=ALU.is_gt, fill=0.0,
                                        base=0, pattern=[[1, P]], channel_multiplier=-1))
        s_const.wait(pool, 0)
        s_const.done(pool.tensor_copy(identb[:, :], ident[:, :]))
        s_const.done(pool.memset(ones[:, :], 1.0))
        s_const.done(pool.memset(zeros[:, :], 0.0))

        steps_self = {"fills": 50, "dve": 40, "act": 5, "pool": 1}
        steps_cross = {"fills": 47, "dve": 51, "act": 5, "pool": 7}
        a1 = Attention(nc, attention, "self", ident[:, :], identb[:, :], HD ** -0.5, steps_self)
        a2 = Attention(nc, attention, "cross", ident[:, :], identb[:, :], 1.0 / D ** 0.5, steps_cross)
        for a in (a1, a2):
            a.slots.prime(nc)
            a.setup(s_const)

        s_const.wait(act, 0)
        act.dma_start(rows[NT * P:NT * P + P, :], zeros[:, :]).then_inc(s_zero, 16)
        act.dma_start(out[NT * P:NT * P + P, :], zeros[:, :]).then_inc(s_zero, 16)

        bank = a2.psum[:, 3, :]
        s_const.wait(pe, 0)
        pe.wait_ge(s_small, 16 * small)
        for c in range(KC):
            for k in range(KC):
                last = pe.transpose(bank[:, (c * KC + k) * P:(c * KC + k + 1) * P], fc_in[:, k, c * P:(c + 1) * P], ident[:, :])
        s_setup.done(last)
        s_setup.wait(v, 0)
        s_setup.done(v.tensor_copy(fc_sb[:, :, :].rearrange("p c n -> p (c n)"), bank))
        v.wait_ge(s_small, 16 * small)
        s_setup.done(v.tensor_scalar(mask_f[:, :], mask_in[:, :], 0.0, None, ALU.not_equal))
        s_setup.wait(pe, 0)
        for c in range(KC):
            pe.transpose(bank[:, c * (E + L):(c + 1) * (E + L)], r_in[:, c * P:(c + 1) * P], ident[0:E + L, 0:E + L])
        s_setup.done(pe.transpose(bank[:, 2 * BANK // 4:2 * BANK // 4 + NT], mask_f[:, :], ident[0:NT, 0:NT]))
        s_setup.wait(v, 0)
        s_setup.done(v.tensor_copy(r_sb[:, :, :].rearrange("p c n -> p (c n)"), bank[:, 0:KC * (E + L)]))
        s_setup.done(v.tensor_copy(keep[:, :], bank[:, 2 * BANK // 4:2 * BANK // 4 + NT]))
        s_setup.wait(v, 0)
        s_setup.done(v.tensor_scalar(drop[:, :], keep[:, :], -1.0, 1.0, ALU.mult, ALU.add))
        s_setup.wait(v, 0)
        for a, part in enumerate(bf16_parts(NEG)):
            s_setup.done(v.tensor_scalar(neg[:, :, a], drop[:, :], part, None, ALU.mult))
        for engine in (v, act, pe, pool):
            s_setup.wait(engine, 0)
            s_const.wait(engine, 0)

        def residual(n):
            return xs[:, bass.ds(n * T, T), :]

        def self_first(n):
            a = a1
            a.start()
            k = layer_norm(nc, n, a.dve, residual(n), a.xn[:, :, :], a.stats)
            yield 4.5
            turned, k_t = a.turn_rows(n, a.xn, a.xnT[:, :, :, :], lambda engine: a.dve.wait(engine, n, k))
            yield 1.3
            turned.wait(pe, n, k_t)
            for t in range(T):
                for lo, width in ((0, 2 * D), (2 * D, D)):
                    i, bank = a.slots.fill(pe, n)
                    for c in range(KC):
                        last = pe.matmul(bank[:, 0:width], a.xnT[:, c, t, :], wqkv[:, c, lo:lo + width],
                                         start=(c == 0), stop=(c == KC - 1))
                    a.slots.filled(i, last)
                    a.slots.take(v, n, i)
                    if lo == 0:
                        o = qk[:, :, t, :]
                        i0 = bank.rearrange("p (w d) -> p w d", w=2)
                        i1 = bias_qkv[:, 0:width].rearrange("p (w d) -> p w d", w=2)
                    else:
                        o = a.v[:, t, :, 0:HD]
                        i0 = bank[:, 0:D].rearrange("p (h d) -> p h d", d=HD)
                        i1 = bias_qkv[:, lo:lo + D].rearrange("p (h d) -> p h d", d=HD)
                    a.slots.taken(i, v.tensor_tensor(o, i0, i1, ALU.add))
                    yield 1.7 if lo == 0 else 0.9
            for s in a.slots.free:
                s.wait(v, n)
            v_step = [(s, s.k) for s in a.slots.free]
            part = qk[:, :, :, :].rearrange("p w t (h d) -> p w t h d", d=HD)[:, :, :, :, 4:12]
            for t in range(T):
                cos = table[:, t, 0, :].rearrange("p (a b d) -> p a b d", a=1, b=1).broadcast_to([P, 2, H, 8])
                a.dve.done(v.tensor_tensor(turn_a[:, :, t], part[:, :, t], cos, ALU.mult))
                for z in range(2):
                    sin = table[:, t, 1, :].rearrange("p (a b d) -> p a b d", a=1, b=1)[:, :, :, z::2]
                    a.dve.done(v.tensor_tensor(turn_b[:, :, t, :, z::2], part[:, :, t, :, 1 - z::2],
                                               sin.broadcast_to([P, 2, H, 4]), ALU.mult))
            a.dve.wait(v, n)
            k_rope = a.dve.done(v.tensor_tensor(part.rearrange("p w t h d -> p (w t h) d"),
                                                turn_a[:, :, :, :, :].rearrange("p w t h d -> p (w t h) d"),
                                                turn_b[:, :, :, :, :].rearrange("p w t h d -> p (w t h) d"), ALU.add))
            a.dve.wait(act, n, k_rope)
            a.dve.wait(v, n, k_rope)
            a.dve.wait(pool, n, k_rope)
            a.pool.done(pool.tensor_tensor(x_bias[:, :, :], residual(n), bias_o[:, :]
                                                    .rearrange("p (a d) -> p a d", a=1).broadcast_to([P, T, D]), ALU.add))
            yield 3.0
            yield from a.split(n, qk[:, 0], qk[:, 1])
            yield from a.stacks(n)
            yield from a.maxima(n)
            a.v_step = v_step

        def self_second(n):
            a = a1
            yield from a.softmax_values(n, lambda engine: [s.wait(engine, n, k) for s, k in a.v_step])
            yield from a.outputs(n, wo_sb)
            i, bank = a.out_slot
            a.pool.wait(v, n, a.pool.per_pass)
            a.slots.take(v, n, i)
            a.slots.taken(i, v.tensor_tensor(residual(n), bank.rearrange("p (t d) -> p t d", t=T),
                                             x_bias[:, :, :], ALU.add))
            yield 2.0
            a.end()

        def cross_first(n):
            a = a2
            a.start()
            for s in a1.slots.free:
                s.wait(v, n, s.per_pass)
            k_norm = layer_norm(nc, n, a.dve, residual(n), a.xn[:, :, :], a.stats)
            a.dve.wait(sp, n, k_norm)
            ctx_load.start()
            ctx_load.done(sp.dma_start(cx[:, :, :], c_t[:, bass.ds(n * T, T), :]))
            a.dve.wait(pool, n, k_norm)
            a.pool.done(pool.tensor_copy(keep_n[:, :], keep[:, bass.ds(n * T, T)]))
            a.pool.wait(pool, n)
            ctx_load.hold(pool, n, idle=a.idle_pool)
            for t in range(T):
                a.pool.done(pool.tensor_scalar(ctx_keep[:, t, :], cx[:, t, :],
                                               keep_n[:, t:t + 1], None, ALU.mult))
            k_keys = a.pool.k
            for t in range(T):
                a.pool.done(pool.tensor_copy(a.v[:, t, :, 0:HD], cx[:, t, :].rearrange("p (h d) -> p h d", d=HD)))
                a.pool.done(pool.tensor_copy(a.parts[1][:, t, :, MASK0:MAX0],
                                             neg[:, bass.ds(n * T + t, 1), :].broadcast_to([P, H, PARTS])))
            k_values = a.pool.k
            yield 4.5
            a.dve.wait(act, n, k_norm)
            a.dve.wait(v, n, k_norm)
            a.pool.wait(act, n, k_keys)
            a.pool.wait(v, n, k_keys)
            yield from a.split(n, a.xn[:, :, :], ctx_keep[:, :, :])
            a.pool.wait(pe, n, k_values)
            yield from a.stacks(n)
            a.k_values = k_values
            yield from a.maxima(n)

        def cross_second(n):
            a = a2
            yield from a.softmax_values(n, lambda engine: a.pool.wait(engine, n, a.k_values))
            yield from a.outputs(n, fc_sb)
            i, bank = a.out_slot
            a.slots.take(v, n, i)
            free, k = a.slots.taken(i, v.tensor_tensor(residual(n), bank.rearrange("p (t d) -> p t d", t=T),
                                                       residual(n), ALU.add))
            free.wait(v, n, k)
            yield 2.0
            k = layer_norm(nc, n, a.dve, residual(n), a.xn[:, :, :], a.stats)
            a.dve.wait(sp, n, k)
            stored.start()
            stored.done(sp.dma_start(out_t[:, bass.ds(n * T, T), :], residual(n)))
            stored.done(sp.dma_start(rows_t[:, bass.ds(n * T, T), :], a.xn[:, :, :]))
            yield 4.5
            turned, k_t = a.turn_rows(n, a.xn, a.xnT[:, :, :, :], lambda engine: a.dve.wait(engine, n, k))
            yield 1.3
            turned.wait(pe, n, k_t)
            i, bank = a.project(n, a.xnT, r_sb, E + L)
            stored.wait(v, n)
            a.slots.take(v, n, i)
            a.slots.taken(i, v.tensor_tensor(
                logits[:, bass.ds(n * T, T), :], bank[:, 0:T * (E + L)].rearrange("p (t e) -> p t e", t=T),
                r_bias[:, :].rearrange("p (a e) -> p a e", a=1).broadcast_to([P, T, E + L]), ALU.add))
            yield 2.0
            a.end()

        v.wait_ge(s_x0, 16)
        interleave(self_first(0))
        interleave(self_second(0))
        v.wait_ge(s_x, 16)
        pool.wait_ge(s_x, 16)
        interleave(self_first(1))
        interleave(self_second(1), cross_first(0))
        with nc.Fori(2, B) as n:
            interleave(chain(self_first(n), self_second(n)), chain(cross_second(n - 2), cross_first(n - 1)))
        interleave(cross_second(B - 2))
        interleave(cross_first(B - 1))
        interleave(cross_second(B - 1))

        for engine in (v, act, pe, pool, sp):
            for s in a2.slots.free:
                s.wait(engine, B - 1, s.per_pass)
            a2.pool.wait(engine, B - 1, a2.pool.per_pass)
        attention.close()
        stored.wait(sp, B - 1, 2)
        stored.wait(pool, B - 1, 2)
        experts(nc, whole, sem, out, rows, logits, ident, upper, ones, w1_sb, s_w1, s_zero, w1, w2, b1, b2)


def route(nc, sb, sem, logits, upper, ones, bank):
    v, pe, pool, act = nc.vector, nc.tensor, nc.gpsimd, nc.scalar
    step = Steps(sem("route"), 0)

    def on(engine, instruction):
        step.done(instruction)
        step.wait(engine, 0)

    def tile(name, *shape, dt=F32):
        return sb(f"route_{name}", [P, *shape], dt)

    def last(ap, width):
        return ap.rearrange("p (t a) -> p t a", a=1).broadcast_to([P, NT, width])

    stat, recip = tile("stat", NT), tile("recip", NT)
    lang = tile("lang", NT, L + 1)
    z, prob = tile("z", NT, E), tile("prob", NT, E)
    hot = [tile(f"hot{i}", NT, E) for i in range(TOPK)]
    top = [tile(f"top{i}", NT) for i in range(TOPK)]
    gate = [tile(f"gate{i}", NT) for i in range(TOPK)]
    work, work2 = tile("work", NT, E), tile("work2", NT, E)
    order_i, order = tile("order_i", E, dt=I32), tile("order", E)
    index_i, index = tile("index_i", N_TILES, dt=I32), tile("index", N_TILES)
    slot_i, slot = tile("slot_i", P, dt=I32), tile("slot", P)
    lane_i, lane = tile("lane_i", 1, dt=I32), tile("lane", 1)
    start = tile("start", N_TILES)
    place, facts = tile("place", E, NT), tile("facts", E, NT, 3 + PARTS, dt=BF16)
    tile_expert = tile("tile_expert", N_TILES, dt=I32)

    on(pool, pool.iota(order_i[:, :], [[-1, E]], base=E, channel_multiplier=0))
    on(pool, pool.iota(index_i[:, :], [[1, N_TILES]], base=0, channel_multiplier=0))
    on(pool, pool.iota(slot_i[:, :], [[1, P]], base=0, channel_multiplier=0))
    on(v, pool.iota(lane_i[:, :], [[0, 1]], base=0, channel_multiplier=1))
    on(v, v.tensor_copy(slot[:, :], slot_i[:, :]))
    on(v, v.tensor_copy(lane[:, :], lane_i[:, :]))
    on(v, v.tensor_copy(order[:, :], order_i[:, :]))
    on(v, v.tensor_copy(index[:, :], index_i[:, :]))

    def softmax(src, width, out):
        on(v, v.tensor_reduce(stat[:, :], src, AXX, ALU.max))
        on(act, v.tensor_tensor(out, src, last(stat[:, :], width), ALU.subtract))
        on(v, act.activation(out, out, ACT.Exp))
        on(v, v.tensor_reduce(stat[:, :], out, AXX, ALU.add))
        on(v, v.reciprocal(recip[:, :], stat[:, :]))
        on(v, v.tensor_tensor(out, out, last(recip[:, :], width), ALU.mult))

    on(v, v.memset(lang[:, :, L:L + 1], 0.0))
    softmax(logits[:, :, E:E + L], L, lang[:, :, 0:L])
    on(v, v.tensor_tensor(work[:, :, 0:L], lang[:, :, 0:L], lang[:, :, 1:L + 1], ALU.add))
    for i in range(E // L):
        on(v, v.scalar_tensor_tensor(out=z[:, :, i * L:(i + 1) * L], in0=work[:, :, 0:L], scalar=0.1,
                                     in1=logits[:, :, i * L:(i + 1) * L], op0=ALU.mult, op1=ALU.add))
    softmax(z[:, :, :], E, prob[:, :, :])

    order_all = order[:, :].rearrange("p (a e) -> p a e", a=1).broadcast_to([P, NT, E])
    for i in range(TOPK):
        on(v, v.tensor_reduce(top[i][:, :], prob[:, :, :], AXX, ALU.max))
        on(v, v.tensor_tensor(work[:, :, :], prob[:, :, :], last(top[i][:, :], E), ALU.is_equal))
        on(v, v.tensor_tensor(work[:, :, :], work[:, :, :], order_all, ALU.mult))
        on(v, v.tensor_reduce(stat[:, :], work[:, :, :], AXX, ALU.max))
        on(v, v.tensor_tensor(hot[i][:, :, :], work[:, :, :], last(stat[:, :], E), ALU.is_equal))
        if i == 0:
            on(v, v.scalar_tensor_tensor(out=prob[:, :, :], in0=hot[0][:, :, :], scalar=-2.0,
                                         in1=prob[:, :, :], op0=ALU.mult, op1=ALU.add))
    on(v, v.tensor_tensor(work2[:, :, :], hot[0][:, :, :], hot[1][:, :, :], ALU.add))
    step.wait(pe, 0)

    chosen = work2[:, :, :].rearrange("p t e -> p (t e)")
    before, total = bank[:, 0:NT * E], bank[:, NT * E:2 * NT * E]
    pe.matmul(before, upper[:, :], chosen, start=True, stop=True)
    on(v, pe.matmul(total, ones[:, :], chosen, start=True, stop=True))

    on(v, v.tensor_tensor(stat[:, :], top[0][:, :], top[1][:, :], ALU.add))
    on(v, v.reciprocal(recip[:, :], stat[:, :]))
    for i in range(TOPK):
        on(v, v.tensor_tensor(gate[i][:, :], top[i][:, :], recip[:, :], ALU.mult))

    sums = [prob, z]
    on(v, v.tensor_copy(work2[:, :, :].rearrange("p t e -> p (t e)"), total))
    on(v, v.tensor_copy(sums[0][:, :, :], work2[:, :, :]))
    for i, d in enumerate((1, 2, 4, 8)):
        a, b = sums[i % 2], sums[1 - i % 2]
        on(v, v.tensor_copy(b[:, 0:d, :], a[:, 0:d, :]))
        on(v, v.tensor_tensor(b[:, d:NT, :], a[:, d:NT, :], a[:, 0:NT - d, :], ALU.add))
    upto = sums[0]
    on(v, v.tensor_tensor(work2[:, :, :], upto[:, :, :], work2[:, :, :], ALU.subtract))

    fill_i, fill_i2 = tile("fill_i", E, dt=I32), tile("fill_i2", E, dt=I32)
    ends = [tile(f"ends{i}", E) for i in range(2)]
    tiles_of, start_row = tile("tiles_of", E), tile("start_row", E)
    on(v, v.tensor_scalar(fill_i[:, :], upto[:, NT - 1, :], float(P - 1), None, ALU.add))
    on(v, v.tensor_scalar(fill_i2[:, :], fill_i[:, :], P.bit_length() - 1, None, ALU.logical_shift_right))
    on(v, v.tensor_copy(tiles_of[:, :], fill_i2[:, :]))
    on(v, v.tensor_copy(ends[0][:, :], tiles_of[:, :]))
    for i, d in enumerate((1, 2, 4)):
        a, b = ends[i % 2], ends[1 - i % 2]
        on(v, v.tensor_copy(b[:, 0:d], a[:, 0:d]))
        on(v, v.tensor_tensor(b[:, d:E], a[:, d:E], a[:, 0:E - d], ALU.add))
    end = ends[1]
    on(v, v.tensor_tensor(start_row[:, :], end[:, :], tiles_of[:, :], ALU.subtract))
    on(v, v.tensor_scalar(start_row[:, :], start_row[:, :], float(P), None, ALU.mult))

    on(v, v.tensor_tensor(work2[:, :, :], work2[:, :, :], start_row[:, :]
                          .rearrange("p (a e) -> p a e", a=1).broadcast_to([P, NT, E]), ALU.add))
    on(v, v.tensor_tensor(work2[:, :, :].rearrange("p t e -> p (t e)"), before,
                          work2[:, :, :].rearrange("p t e -> p (t e)"), ALU.add))
    by_expert = work2[:, :, :].rearrange("p t e -> p e t")
    chosen_by = [x[:, :, :].rearrange("p t e -> p e t") for x in hot]
    on(v, v.tensor_scalar(work2[:, :, :], work2[:, :, :], 1.0, None, ALU.add))
    on(v, v.tensor_tensor(place[:, :, :], chosen_by[0], chosen_by[1], ALU.add))
    on(v, v.tensor_tensor(place[:, :, :], place[:, :, :], by_expert, ALU.mult))
    on(v, v.tensor_scalar(place[:, :, :], place[:, :, :], -1.0, None, ALU.add))

    for i in range(TOPK):
        on(v, v.tensor_tensor(hot[i][:, :, :], hot[i][:, :, :], last(gate[i][:, :], E), ALU.mult))
    on(v, v.tensor_tensor(work[:, :, :], hot[0][:, :, :], hot[1][:, :, :], ALU.add))
    rest = work[:, :, :].rearrange("p t e -> p e t")
    for a in range(PARTS):
        on(v, v.tensor_copy(facts[:, :, :, 3 + a], rest))
        if a + 1 < PARTS:
            on(v, v.tensor_tensor(rest, rest, facts[:, :, :, 3 + a], ALU.subtract))
    on(v, v.memset(facts[:, :, :, 0], 1.0))
    on(v, v.tensor_copy(facts[:, :, :, 1], lane[:, :].rearrange("p (a b) -> p a b", a=1)
                        .broadcast_to([P, E, NT])))
    on(v, v.tensor_copy(facts[:, :, :, 2], index[:, 0:NT].rearrange("p (a b) -> p a b", a=1)
                        .broadcast_to([P, E, NT])))

    past = tile("past", N_TILES, E)
    on(v, v.tensor_tensor(past[:, :, :],
                          index[:, :].rearrange("p (j a) -> p j a", a=1).broadcast_to([P, N_TILES, E]),
                          end[:, :].rearrange("p (a e) -> p a e", a=1).broadcast_to([P, N_TILES, E]), ALU.is_ge))
    on(v, v.tensor_scalar(start[:, :], index[:, :], float(P), None, ALU.mult))
    on(v, v.tensor_reduce(index[:, :], past[:, :, :], AXX, ALU.add))
    step.done(v.tensor_scalar(tile_expert[:, :], index[:, :], float(E - 1), None, ALU.min))
    return step, place, facts, tile_expert, start, slot, lane


def experts(nc, whole, sem, out, rows, logits, ident, upper, ones, w1_sb, s_w1, s_zero, w1, w2, b1, b2):
    v, act, pe, pool, sp = nc.vector, nc.scalar, nc.tensor, nc.gpsimd, nc.sync

    def sb(name, shape, dt=F32):
        return whole.enter_context(nc.sbuf_tensor(name, shape, dt))

    s_b, s_w1b, s_w2, s_b2 = (sem(f"load_{w}") for w in ("b1", "w1b", "w2", "b2"))
    w1_sb.append(sb("w1_sb1", [P, E, F]))
    w2_sb = sb("w2_sb", [P, E, FC, D])
    b1_in, b1_sb = sb("b1_in", [E * FC, P]), sb("b1_sb", [P, E, FC])
    b2_sb = sb("b2_sb", [P, E, D])
    sp.wait_ge(s_zero, 16 * 2)
    sp.dma_start(b1_in[:, :], b1.rearrange("e (c p) -> (e c) p", p=P)).then_inc(s_b, 16)
    for e in range(E):
        sp.dma_start(w1_sb[1][:, e, :], w1[e, P:2 * P, :]).then_inc(s_w1b, 16)
    for e in range(E):
        sp.dma_start(w2_sb[:, e, :, :], w2[e].rearrange("(c p) d -> p c d", p=P)).then_inc(s_w2, 16)
    for e in range(E):
        sp.dma_start(b2_sb[:, e, :], b2[e:e + 1, :].broadcast_to([P, D])).then_inc(s_b2, 16)

    psum = whole.enter_context(nc.psum_tensor("experts_psum", [P, 7, BANK], F32))
    h_bank, hT_bank = (psum[:, b:b + 2, :].rearrange("p b n -> p (b n)") for b in (0, 2))
    x_bank, y_bank, fact_bank = psum[:, 4, :], psum[:, 5, :], psum[:, 6, :]

    s_bias = Steps(sem("bias"), 0)
    pe.wait_ge(s_b, 16)
    s_bias.done(pe.transpose(x_bank[:, 0:E * FC], b1_in[:, :], ident[0:E * FC, 0:E * FC]))

    step, place, facts, tile_expert, start, slot, lane = route(nc, sb, sem, logits, upper, ones, y_bank)
    s_bias.wait(v, 0)
    s_bias.done(v.tensor_copy(b1_sb[:, :, :].rearrange("p e c -> p (e c)"), x_bank[:, 0:E * FC]))

    beyond = sb("beyond", [P, 1])
    near, hit = sb("near", [P, NT]), sb("hit", [P, NT, P], BF16)
    found, spare, token_f = sb("found", [P, 3 + PARTS]), sb("spare", [P, 1]), sb("token_f", [P, 1])
    gate, gates = sb("gate", [P, 1]), sb("gates", [P, N_TILES])
    token, token_out, tokens = sb("token", [P, 1], I32), sb("token_out", [P, 1], I32), sb("tokens", [P, N_TILES], I32)
    x_rows, xT = sb("x_rows", [P, D]), sb("xT", [P, KC, P])
    hid, hidT, y, y_gated = sb("hid", [P, F]), sb("hidT", [P, FC, P]), sb("y", [P, D]), sb("y_gated", [P, D])
    (s_near, s_hit, s_fact, s_found, s_sum1, s_sum2, s_token, s_gather, s_turned_x, s_moved_x, s_up, s_moved_h,
     s_turned_h, s_gelu, s_down, s_moved_y, s_gated, s_add) = (
        Steps(sem(f"tile_{w}"), 1, by=16 if w in ("gather", "add") else 1) for w in
        ("near", "hit", "fact", "found", "sum1", "sum2", "token", "gather", "turned_x", "moved_x", "up", "moved_h",
         "turned_h", "gelu", "down", "moved_y", "gated", "add"))

    idle = sem("idle_tiles")

    def once(steps, instruction):
        steps.start()
        steps.done(instruction)

    def after(engine, steps, j):
        if not (isinstance(j, int) and j < 0):
            steps.wait(engine, j, 1)

    def expert_of(engine, j):
        return engine.value_load(tile_expert[0:1, bass.ds(j, 1)], min_val=0, max_val=E - 1)

    def hits(j):
        e = expert_of(v, j)
        once(s_near, v.tensor_scalar(near[:, :], place[:, bass.ds(e, 1), :].rearrange("p a t -> p (a t)"),
                                     start[:, bass.ds(j, 1)], None, ALU.subtract))
        after(v, s_near, j)
        after(v, s_fact, j - 1)
        once(s_hit, v.tensor_tensor(
            hit[:, :, :], slot[:, :].rearrange("p (a s) -> p a s", a=1).broadcast_to([P, NT, P]),
            near[:, :].rearrange("p (t a) -> p t a", a=1).broadcast_to([P, NT, P]), ALU.is_equal))

    def fact(j):
        e = expert_of(pe, j)
        after(pe, s_hit, j)
        after(pe, s_found, j - 1)
        for t in range(NT):
            last = pe.matmul(fact_bank[:, 0:3 + PARTS], hit[:, t, :],
                             facts[:, bass.ds(e, 1), t, :].rearrange("p a c -> p (a c)"),
                             start=(t == 0), stop=(t == NT - 1))
        once(s_fact, last)
        after(v, s_fact, j)
        once(s_found, v.tensor_copy(found[:, :], fact_bank[:, 0:3 + PARTS]))
        after(v, s_found, j)
        v.scalar_tensor_tensor(out=token_f[:, :], in0=found[:, 2:3], scalar=float(P), in1=found[:, 1:2],
                               op0=ALU.mult, op1=ALU.add)
        v.tensor_scalar(spare[:, :], found[:, 0:1], -1.0, 1.0, ALU.mult, ALU.add)
        once(s_sum1, v.tensor_tensor(gate[:, :], found[:, 3:4], found[:, 4:5], ALU.add))
        after(v, s_sum1, j)
        once(s_sum2, v.tensor_tensor(spare[:, :], spare[:, :], beyond[:, :], ALU.mult))
        after(v, s_sum2, j)
        after(v, s_gather, j - 1)
        v.tensor_tensor(tokens[:, bass.ds(j, 1)], token_f[:, :], spare[:, :], ALU.add)
        v.tensor_tensor(gates[:, bass.ds(j, 1)], gate[:, :], found[:, 5:6], ALU.add)
        once(s_token, v.tensor_tensor(token[:, :], token_f[:, :], spare[:, :], ALU.add))

    def gather(j):
        after(pool, s_token, j)
        after(pool, s_turned_x, j - 1)
        pool.sem_inc(idle, 1)
        once(s_gather, pool.indirect_dma_start(
            out=x_rows[:, :], out_offset=None, in_=rows,
            in_offset=bass.IndirectOffsetOnAxis(ap=token[:, :].bitcast(U32), axis=0)))

    def turn_x(j):
        after(pe, s_gather, j)
        after(pe, s_moved_x, j - 1)
        for c in range(KC):
            last = pe.transpose(x_bank[:, c * P:(c + 1) * P], x_rows[:, c * P:(c + 1) * P], ident[:, :])
        once(s_turned_x, last)
        after(act, s_turned_x, j)
        after(act, s_up, j - 1)
        once(s_moved_x, act.copy(xT[:, :, :].rearrange("p c t -> p (c t)"), x_bank[:, 0:D]))

    def up_layer(j):
        e = expert_of(pe, j)
        after(pe, s_moved_x, j)
        after(pe, s_moved_h, j - 1)
        for half in range(F // BANK):
            for c in range(KC):
                last = pe.matmul(h_bank[:, half * BANK:(half + 1) * BANK], xT[:, c, :],
                                 w1_sb[c][:, bass.ds(e, 1), half * BANK:(half + 1) * BANK]
                                 .rearrange("p a n -> p (a n)"), start=(c == 0), stop=(c == KC - 1))
        once(s_up, last)
        after(v, s_up, j)
        after(v, s_turned_h, j - 1)
        once(s_moved_h, v.tensor_copy(hid[:, :], h_bank))

    def turn_h(j):
        after(pe, s_moved_h, j)
        after(pe, s_gelu, j - 1)
        for c in range(FC):
            last = pe.transpose(hT_bank[:, c * P:(c + 1) * P], hid[:, c * P:(c + 1) * P], ident[:, :])
        once(s_turned_h, last)
        e = expert_of(act, j)
        after(act, s_turned_h, j)
        after(act, s_down, j - 1)
        for c in range(FC):
            last = act.activation(hidT[:, c, :], hT_bank[:, c * P:(c + 1) * P], ACT.Gelu,
                                  bias=b1_sb[:, bass.ds(e, 1), c])
        once(s_gelu, last)

    def down_layer(j):
        e = expert_of(pe, j)
        after(pe, s_gelu, j)
        after(pe, s_moved_y, j - 1)
        for c in range(FC):
            last = pe.matmul(y_bank[:, 0:D], hidT[:, c, :],
                             w2_sb[:, bass.ds(e, 1), c, :].rearrange("p a n -> p (a n)"),
                             start=(c == 0), stop=(c == FC - 1))
        once(s_down, last)
        e = expert_of(v, j)
        after(v, s_down, j)
        after(v, s_gated, j - 1)
        once(s_moved_y, v.tensor_tensor(y[:, :], y_bank[:, 0:D],
                                        b2_sb[:, bass.ds(e, 1), :].rearrange("p a n -> p (a n)"), ALU.add))
        after(v, s_moved_y, j)
        after(v, s_add, j - 1)
        v.tensor_copy(token_out[:, :], tokens[:, bass.ds(j, 1)])
        once(s_gated, v.tensor_scalar(y_gated[:, :], y[:, :], gates[:, bass.ds(j, 1)], None, ALU.mult))
        after(pool, s_gated, j)
        pool.sem_inc(idle, 1)
        once(s_add, pool.indirect_dma_start(
            out=out, out_offset=bass.IndirectOffsetOnAxis(ap=token_out[:, :].bitcast(U32), axis=0),
            in_=y_gated[:, :], in_offset=None, compute_op=ALU.add))

    on_start = Steps(sem("tiles_start"), 0)
    step.wait(v, 0)
    on_start.done(v.tensor_scalar(beyond[:, :], lane[:, :], float(NT * P), None, ALU.add))
    for engine in (v, act, pe, pool):
        step.wait(engine, 0)
        s_bias.wait(engine, 0)
        on_start.wait(engine, 0)
    pool.wait_ge(s_zero, 16 * 2)

    def tick(j):
        for what, ahead in ((fact, 3), (turn_h, 0), (hits, 4), (up_layer, 1), (gather, 3), (turn_x, 2),
                            (down_layer, 0)):
            if not isinstance(j, int) or 0 <= j + ahead < N_TILES:
                what(j + ahead)

    for j in range(-4, -1):
        tick(j)
    pe.wait_ge(s_w1, 16 * E)
    pe.wait_ge(s_w1b, 16 * E)
    tick(-1)
    pe.wait_ge(s_w2, 16 * E)
    v.wait_ge(s_b2, 16 * E)
    tick(0)
    with nc.Fori(1, N_TILES - 4) as j:
        tick(j)
    for j in range(N_TILES - 4, N_TILES):
        tick(j)
    s_add.wait(pool, N_TILES - 1, 1)


_INS = ["x", "ctx_1024", "mask_Bx1x1xS2_ik0", "L0_attn_Wq", "L0_attn_bq", "L0_attn_Wk", "L0_attn_bk",
        "L0_attn_Wv", "L0_attn_bv", "L0_attn_Wo", "L0_attn_bo", "L0_xattn_W_fc", "L0_ffn_router_w",
        "L0_ffn_router_b", "L0_ffn_lang_w", "L0_ffn_lang_b", "L0_ffn_w1", "L0_ffn_b1", "L0_ffn_w2",
        "L0_ffn_b2"]


def kernel(**inputs):
    import concourse.bacc as bacc
    from concourse.bass_utils import run_bass_kernel_spmd

    nc = bacc.Bacc("TRN2", target_bir_lowering=False, num_devices=1)
    arrays = {f"in_{name}": np.ascontiguousarray(inputs[name]) for name in _INS}
    arrays["rope"] = rope_tables()
    args = [nc.dram_tensor(name, a.shape, mybir.dt.from_np(a.dtype), kind="ExternalInput").ap()
            for name, a in arrays.items()]
    out = nc.dram_tensor("out", (B * S + P, D), F32, kind="ExternalOutput").ap()
    build(nc, *args, out)
    r = run_bass_kernel_spmd(nc, [arrays], core_ids=[0])
    return r.results[0]["out"][:B * S].reshape(B, S, D)
```

```python
from contextlib import ExitStack

import numpy as np

import concourse.bass as bass
from concourse import mybir

F32 = mybir.dt.float32
BF16 = mybir.dt.bfloat16
I32 = mybir.dt.int32
U32 = mybir.dt.uint32
ALU = mybir.AluOpType
ACT = mybir.ActivationFunctionType
AXX = mybir.AxisListType.X

P = 128
B, S, D = 8, 256, 256
H, HD = 16, 16
T = S // P
KC = D // P
NT = B * T
PARTS = 3
Q_PARTS = (0, 0, 0, 1, 1, 2)
K_PARTS = (0, 1, 2, 0, 1, 0)
STACK = 6 * HD
MASK0 = STACK
MAX0 = STACK + PARTS
ROWS = STACK + 2 * PARTS
VW = 32
BANK = 512
MAX_PARTS = 9
NEG = -1e20
EPS = 1e-5
E, L, TOPK, F = 8, 4, 2, 1024
FC = F // P
N_TILES = (NT * P * TOPK - E) // P + E
RSQRT_MAGIC = 0x5F3759DF
COST = {
    "stat": [("dve", 0.14), ("", 0.12)], "norm": [("dve", 0.5), ("", 0.03)],
    "turn": [("pe", 0.52), ("act", 1.2)], "qk": [("pe", 0.86), ("dve", 0.82)], "rope": [("dve", 0.78)],
    "round": [("act", 1.43)], "rest": [("dve", 0.45), ("act", 0.46), ("dve", 0.15)], "again": [("dve", 0.56)],
    "stackq": [("pe", 0.15), ("act", 0.55)],
    "stackk": [("pe", 0.34), ("act", 0.97)], "max": [("pe", 0.18), ("dve", 1.03)],
    "max_turn": [("pe", 0.17), ("dve", 0.38)], "max_dma": [("", 6)], "v": [("pe", 0.99), ("dve", 0.55)],
    "score": [("pe", 0.21), ("act", 0.6)], "values": [("pe", 0.86)], "o_move": [("act", 0.88), ("", 0.09)],
    "normal": [("pe", 1.56), ("dve", 0.25)], "project": [("pe", 1.21), ("dve", 0.84)], "keys": [("", 2.92)],
    "lag_self_front": [("", 13.35)], "lag_half": [("", 2.13)], "lag_cross": [("", 0)], "load": [("", 3)],
    "lag_keys": [("", 5.15)], "lag_setup": [("", 19.43)], "setup": [("pe", 0.78), ("dve", 1.37)],
    "stackv": [("pe", 0.19), ("dve", 0.7)], "behind": [("", 0.84)],
    "delays": [("self_early", 1), ("cross_late", 1), ("self_late", 1.26),
               ("cross_early", 1), ("keys", 0.65), ("self_front", 1)]}


def bf16_parts(value):
    rest, out = np.array([value], np.float32), []
    for _ in range(PARTS):
        part = (rest.view(np.uint32) & np.uint32(0xFFFF0000)).view(np.float32)
        out.append(float(part[0]))
        rest = rest - part
    return out


class Steps:

    def __init__(self, sem, per_pass, credit=0, by=1):
        self.sem, self.per_pass, self.credit, self.by, self.k = sem, per_pass, credit, by, 0

    def start(self):
        self.k = 0

    def end(self):
        assert self.k == self.per_pass, (self.sem.name, self.k, self.per_pass)

    def done(self, instruction):
        self.k += 1
        instruction.then_inc(self.sem, self.by)
        return self.k

    def wait(self, engine, n, k=None):
        k = self.k if k is None else k
        engine.wait_ge(self.sem, (n * self.per_pass + k) * self.by + self.credit)

    def hold(self, engine, n, k=None, idle=None):
        self.wait(engine, n, k)
        engine.sem_inc(idle, 1)


class Arena:

    def __init__(self, whole, spare):
        self.whole, self.used, self.spare = whole, 0, spare

    def __call__(self, name, shape, dt=F32):
        n = int(np.prod(shape[1:])) * (2 if dt == BF16 else 4) // 4
        if self.used + n > self.whole.shape[1]:
            return self.spare(name, shape, dt)
        flat = self.whole[0:shape[0], self.used:self.used + n]
        self.used += n
        flat = flat if dt == F32 else flat.bitcast(dt)
        dims = "abcd"[:len(shape) - 1]
        return flat.rearrange(f"p ({' '.join(dims)}) -> p {' '.join(dims)}", **dict(zip(dims, shape[1:])))


class Turns:

    def __init__(self, sem):
        self.sem, self.counts, self.rings = sem, [], []
        self.m, self.first, self.skipped = None, 0, 0

    def count(self, name, by=1):
        self.counts.append(Count(self, self.sem(name), by))
        return self.counts[-1]

    def reached(self, count, value):
        if self.m is None:
            return value + self.skipped * count.per_turn
        if count.per_turn == 0:
            return value
        return self.m * count.per_turn + (value - self.first * count.per_turn)

    def begin(self):
        for count in self.counts:
            count.before = count.value
        for ring in self.rings:
            ring.unit = 0

    def repeat(self, nc, first, end, turn):
        for count in self.counts:
            count.per_turn = count.value - count.before
        self.first = first
        with nc.Fori(first, end) as self.m:
            turn(self.m, first)
        assert all(count.value - count.before == count.per_turn for count in self.counts)
        self.m, self.skipped = None, end - 1 - first


class Count:

    def __init__(self, turns, sem, by):
        self.turns, self.sem, self.by = turns, sem, by
        self.value = self.before = self.per_turn = 0

    def done(self, instruction):
        instruction.then_inc(self.sem, self.by)
        self.value += self.by
        return self, self.value


def after(engine, *steps):
    latest = {}
    for count, value in filter(None, steps):
        latest[count] = max(value, latest.get(count, 0))
    for count, value in latest.items():
        engine.wait_ge(count.sem, count.turns.reached(count, value))


class Ring:

    def __init__(self, turns, name, banks):
        self.full = [turns.count(f"{name}_full{i}") for i in range(len(banks))]
        self.free = [turns.count(f"{name}_free{i}") for i in range(len(banks))]
        self.filled_by, self.emptied_by = [None] * len(banks), [None] * len(banks)
        self.banks, self.unit = banks, 0
        turns.rings.append(self)

    def fill(self, pe, *steps):
        i = self.unit % len(self.banks)
        self.unit += 1
        assert self.filled_by[i] is None, "in use"
        after(pe, self.emptied_by[i], *steps)
        return i, self.banks[i]

    def filled(self, i, instruction):
        self.filled_by[i] = self.full[i].done(instruction)

    def take(self, engine, i, *steps):
        after(engine, self.filled_by[i], *steps)

    def taken(self, i, instruction):
        self.filled_by[i] = None
        self.emptied_by[i] = self.free[i].done(instruction)
        return self.emptied_by[i]


def layer_norm(nc, dve, src, dst, st, *steps):
    v = nc.vector
    after(v, *steps)
    v.sem_inc(st["idle"], 1)
    for t in range(T):
        k = dve.done(v.bn_stats(st["bn"][:, t, :], src[:, t, :]))
    yield COST["stat"]
    after(v, k)
    v.sem_inc(st["idle"], 1)
    for t in range(T):
        k = dve.done(v.bn_aggr(st["mv"][:, t, :], st["bn"][:, t, :]))
    yield COST["stat"]
    var, y, w = st["var"][:, :], st["rstd"][:, :], st["tmp"][:, :]

    def then(op, *args, **kw):
        nonlocal k
        after(v, k)
        k = dve.done(op(*args, **kw))

    then(v.tensor_scalar, var, st["mv"][:, :, 1], EPS, None, ALU.add)
    yield COST["stat"]
    then(v.tensor_scalar, w.bitcast(I32), var.bitcast(I32), 1, None, ALU.logical_shift_right)
    yield COST["stat"]
    then(v.tensor_scalar, y.bitcast(I32), w.bitcast(I32), -1, float(RSQRT_MAGIC), ALU.mult, ALU.add)
    yield COST["stat"]
    for _ in range(3):
        then(v.tensor_tensor, w, y, y, ALU.mult)
        yield COST["stat"]
        then(v.scalar_tensor_tensor, out=w, in0=w, scalar=-0.5, in1=var, op0=ALU.mult, op1=ALU.mult)
        yield COST["stat"]
        then(v.scalar_tensor_tensor, out=y, in0=w, scalar=1.5, in1=y, op0=ALU.add, op1=ALU.mult)
        yield COST["stat"]
    after(v, k)
    for t in range(T):
        k = dve.done(v.tensor_scalar(dst[:, t, :], src[:, t, :], st["mv"][:, t, 0:1], y[:, t:t + 1],
                                     ALU.subtract, ALU.mult))
    yield COST["norm"]
    return k


class Attention:

    def __init__(self, nc, sb_of, turns, ring, name, o_bank, ident, identb, scale):
        self.nc, self.name, self.scale, self.ident, self.identb = nc, name, scale, ident, identb

        def sb(what, shape, dt=F32):
            return sb_of(f"{name}_{what}", shape, dt)

        self.ring = ring
        self.o_psum = o_bank
        self.dve, self.act, self.pool = (turns.count(f"{name}_{w}") for w in ("dve", "act", "pool"))
        self.pv = turns.count(f"{name}_pv")
        self.max_dma = turns.count(f"{name}_max_dma", by=16)
        self.idle = {w: turns.sem(f"{name}_idle_{w}") for w in ("dve", "pool", "sp")}
        self.at = {}

        def stats(w):
            return {"bn": sb(f"bn{w}", [P, T, 6]), "mv": sb(f"mv{w}", [P, T, 2]), "var": sb(f"var{w}", [P, T]),
                    "rstd": sb(f"rstd{w}", [P, T]), "tmp": sb(f"tmp{w}", [P, T]), "idle": self.idle["dve"]}

        self.xn = sb("xn", [P, T, D])
        self.rest = sb("rest", [P, 2, T, D])
        self.parts = [sb(f"parts_{w}", [P, T, H, ROWS], BF16) for w in "qk"]
        self.stack = [sb(f"stack_{w}", [ROWS, H, T, P], BF16) for w in "qk"]
        self.v = sb("v", [P, T, H, VW])
        self.p = sb("p", [P, 2, BANK])
        self.p_used = [None, None]
        self.o_moved = None
        self.oT = sb("oT", [P, 4, S])
        self.ctx = sb("ctx", [P, T, D])
        self.ctxT = sb("ctxT", [P, KC, T, P])
        self.rden = sb("rden", [P, T, H])
        self.neg_max = sb("neg_max", [P, T, H])
        self.max_rest = sb("max_rest", [P, T, H])
        self.max_parts = sb("max_parts", [P, 2, T, MAX_PARTS, H // 2], BF16)
        self.maxT = sb("maxT", [PARTS * H // 2, 2, T, P], BF16)
        self.stats, self.stats_out = stats(0), stats(1)

    def step(self, what, k):
        return self.at[what, k] if k >= 0 else None

    def until(self, *whats_and_k):
        while any(k >= 0 and (what, k) not in self.at for what, k in whats_and_k):
            yield COST["behind"]

    def setup(self, count):
        nc = self.nc
        q, k = self.parts
        count.done(nc.gpsimd.memset(self.max_parts[:, :, :, :, :], 0.0))
        for what, value in ((q[:, :, :, MASK0:MAX0], 1.0), (q[:, :, :, MAX0:ROWS], 0.0),
                            (k[:, :, :, MASK0:MAX0], 0.0), (k[:, :, :, MAX0:ROWS], 1.0),
                            (self.v[:, :, :, HD:HD + 1], 1.0), (self.v[:, :, :, HD + 1:VW], 0.0)):
            count.done(nc.gpsimd.memset(what, value))

    def turn_rows(self, rows, turned, written, used=()):
        nc = self.nc
        i, bank = self.ring.fill(nc.tensor, *written)
        for c in range(KC):
            for t in range(T):
                last = nc.tensor.transpose(bank[:, (c * T + t) * P:(c * T + t + 1) * P],
                                           rows[:, t, c * P:(c + 1) * P], self.ident)
        self.ring.filled(i, last)
        self.ring.take(nc.scalar, i, *used)
        return self.ring.taken(i, nc.scalar.copy(turned[:, :, :, :].rearrange("p c t q -> p (c t q)"), bank))

    def split(self, k, w, x, *steps):
        nc, dve, act = self.nc, self.dve, self.act
        src = x.rearrange("p t (h d) -> p (t h) d", d=HD)
        rest = self.rest[:, w].rearrange("p t (h d) -> p (t h) d", d=HD)
        dst = self.parts[w].rearrange("p t h r -> p (t h) r")
        order = (Q_PARTS, K_PARTS)[w]

        def block(part):
            b = order.index(part)
            return dst[:, :, b * HD:(b + 1) * HD]

        def again(part):
            at = [b for b in range(6) if order[b] == part]
            blocks = dst[:, :, 0:STACK].rearrange("p g (b d) -> p g b d", d=HD)
            return dve.done(nc.vector.tensor_copy(
                blocks[:, :, at[1]:at[-1] + 1:at[-1] - at[-2], :],
                blocks[:, :, at[0]:at[0] + 1, :].broadcast_to([P, T * H, len(at) - 1, HD])))

        yield from self.until((("stacked", w), k - 1))
        before = self.step(("stacked", w), k - 1)
        after(nc.scalar, before, *steps)
        rounded = act.done(nc.scalar.copy(block(0), src))
        yield COST["round"]
        after(nc.vector, rounded, before, self.step(("third", w), k - 1), *steps)
        k_rest = dve.done(nc.vector.tensor_tensor(rest, src, block(0), ALU.subtract))
        after(nc.scalar, k_rest)
        rounded_rest = act.done(nc.scalar.copy(block(1), rest))
        yield COST["rest"]
        again(0)
        yield COST["again"]
        after(nc.gpsimd, rounded_rest, before)
        nc.gpsimd.sem_inc(self.idle["pool"], 1)
        self.at[("third", w), k] = self.pool.done(nc.gpsimd.tensor_tensor(block(2), rest, block(1), ALU.subtract))
        after(nc.vector, rounded_rest)
        self.at[("split", w), k] = again(1)
        yield COST["again"]

    def stack_and_max(self, k, half):
        nc, v, pe = self.nc, self.nc.vector, self.nc.tensor
        ring, dve = self.ring, self.dve
        qs, ks = self.stack
        stacked = {}
        for g in (2 * half, 2 * half + 1):
            for w in range(2):
                i, bank = ring.fill(pe, self.step(("split", w), k), self.step(("third", w), k))
                turned = bank.bitcast(BF16)
                for j in range(4):
                    for t in range(T):
                        last = pe.transpose(turned[0:ROWS, (j * T + t) * P:(j * T + t + 1) * P],
                                            self.parts[w][:, t, 4 * g + j, :], self.identb)
                ring.filled(i, last)
                on_v = self.name == "self" and g == 0 and w == 0
                ring.take(nc.vector if on_v else nc.scalar, i)
                copy = nc.vector.tensor_copy if on_v else nc.scalar.copy
                out = self.stack[w][:, 4 * g:4 * g + 4].rearrange("r h t p -> r (h t p)")
                stacked[g, w] = ring.taken(i, copy(out, turned[0:ROWS, :]))
                if g == 3:
                    self.at[("stacked", w), k] = stacked[g, w]
                yield COST["stackv" if on_v else "stack" + "qk"[w]]
        heads, maxima = range(half * H // 2, (half + 1) * H // 2), []
        for h in heads:
            i, bank = ring.fill(pe, *([stacked[h // 4, w] for w in range(2)] if h % 4 == 0 else ()))
            for t in range(T):
                last = pe.matmul(bank[:, t * S:(t + 1) * S], qs[0:MAX0, h, t, :],
                                 ks[0:MAX0, h].rearrange("r t p -> r (t p)"), start=True, stop=True)
            ring.filled(i, last)
            ring.take(v, i)
            maxima.append(ring.taken(i, v.tensor_reduce(self.neg_max[:, :, h:h + 1],
                                                        bank.rearrange("p (t k) -> p t k", t=T),
                                                        AXX, ALU.max, negate=True)))
            yield COST["max"]
        mp = self.max_parts[:, half]
        neg_max, rest = (x[:, :, heads[0]:heads[-1] + 1] for x in (self.neg_max, self.max_rest))
        after(v, *maxima)
        k_mp = dve.done(v.tensor_copy(mp[:, :, 0, :], neg_max))
        yield COST["stat"]
        after(v, k_mp)
        k_mp = dve.done(v.tensor_tensor(rest, neg_max, mp[:, :, 0, :], ALU.subtract))
        yield COST["stat"]
        after(v, k_mp)
        k_mp = dve.done(v.tensor_copy(mp[:, :, 1, :], rest))
        yield COST["stat"]
        after(v, k_mp)
        k_mp = dve.done(v.tensor_tensor(mp[:, :, 2, :], rest, mp[:, :, 1, :], ALU.subtract))
        yield COST["stat"]
        i, bank = ring.fill(pe, k_mp)
        turned = bank.bitcast(BF16)
        for t in range(T):
            last = pe.transpose(turned[0:MAX_PARTS * H // 2, t * P:(t + 1) * P],
                                mp[:, t].rearrange("p a h -> p (a h)"), self.identb)
        ring.filled(i, last)
        ring.take(v, i)
        written = ring.taken(i, v.tensor_copy(self.maxT[:, half].rearrange("r t p -> r (t p)"),
                                              turned[0:PARTS * H // 2, 0:S]))
        after(nc.sync, written)
        for a in range(PARTS):
            self.at[("max", half), k] = self.max_dma.done(
                nc.sync.dma_start(qs[MAX0 + a:MAX0 + a + 1, heads[0]:heads[-1] + 1],
                                  self.maxT[a * H // 2:(a + 1) * H // 2, half]))
        yield COST["max_turn"]

    def softmax_values(self, k, half, lag):
        nc, pe, act, v = self.nc, self.nc.tensor, self.nc.scalar, self.nc.vector
        ring = self.ring
        qs, ks = self.stack
        exp_done = {}
        heads = range(half * H // 2, (half + 1) * H // 2)
        yield lag

        def scores(h):
            i, bank = ring.fill(pe, self.step(("max", half), k) if h == heads[0] else None)
            for t in range(T):
                last = pe.matmul(bank[:, t * S:(t + 1) * S], ks[:, h, t, :],
                                 qs[:, h].rearrange("r t p -> r (t p)"), start=True, stop=True)
            ring.filled(i, last)
            ring.take(act, i, self.p_used[h % 2])
            exp_done[h] = ring.taken(i, act.activation(self.p[:, h % 2, :], bank, ACT.Exp, scale=self.scale))

        def values(h):
            after(pe, exp_done[h], *([self.o_moved] + [self.step(("v", t), k) for t in range(T)]
                                    if h == heads[0] else []))
            g, j = h // 4, h % 4
            out = self.o_psum[32 * j:32 * j + 32, (g % 2) * S:(g % 2 + 1) * S]
            for t in range(T):
                last = pe.matmul(out, self.v[:, t, h, :], self.p[:, h % 2, t * S:(t + 1) * S],
                                 start=(t == 0), stop=(t == T - 1))
            self.p_used[h % 2] = self.pv.done(last)

        scores(heads[0])
        yield COST["score"]
        for h in heads:
            if h < heads[-1]:
                scores(h + 1)
                yield COST["score"]
            values(h)
            yield COST["values"]
        yield from self.until(("ctx", k - 1))
        after(act, self.p_used[heads[-1] % 2], self.step("ctx", k - 1))
        self.o_moved = self.act.done(act.copy(
            self.oT[:, 2 * half:2 * half + 2, :].rearrange("p g s -> p (g s)"), self.o_psum))
        yield COST["o_move"]

    def outputs(self, k, weight, o_moved):
        nc, pe, v = self.nc, self.nc.tensor, self.nc.vector
        ring, dve, written = self.ring, self.dve, []
        for t in range(T):
            i, bank = ring.fill(pe, o_moved)
            for g in range(4):
                last = pe.transpose(bank[:, g * P:(g + 1) * P], self.oT[:, g, t * P:(t + 1) * P], self.ident)
            ring.filled(i, last)
            ring.take(v, i)
            heads = bank.rearrange("p (h w) -> p h w", w=VW)
            rden = self.rden[:, t, :].rearrange("p (h a) -> p h a", a=1)
            k_rden = dve.done(v.reciprocal(rden, heads[:, :, HD:HD + 1]))
            after(v, k_rden)
            written.append(ring.taken(i, v.tensor_tensor(
                self.ctx[:, t, :].rearrange("p (h d) -> p h d", d=HD), heads[:, :, 0:HD],
                rden.broadcast_to([P, H, HD]), ALU.mult)))
            yield COST["normal"]
        self.at["ctx", k] = written[-1]
        turned = self.turn_rows(self.ctx, self.ctxT, written)
        yield COST["turn"]
        return self.project(self.ctxT, weight, D, turned)

    def project(self, rowsT, weight, width, *steps):
        pe = self.nc.tensor
        i, bank = self.ring.fill(pe, *steps)
        for t in range(T):
            for c in range(KC):
                last = pe.matmul(bank[:, t * width:(t + 1) * width], rowsT[:, c, t, :], weight[:, c, :],
                                 start=(c == 0), stop=(c == KC - 1))
        self.ring.filled(i, last)
        return i, bank


def queue(*passes):
    free = {}
    running = [{"at": 0.0, "delay": delay, "steps": p, "parent": None} for delay, p in passes]
    while running:
        task = min(running, key=lambda task: task["at"] + task["delay"])
        step = next(task["steps"], None)
        if step is None:
            running.remove(task)
            parent = task["parent"]
            if parent:
                parent["at"] = max(parent["at"], task["at"])
                parent["waits"] -= 1
                if not parent["waits"]:
                    running.append(parent)
        elif isinstance(step, tuple):
            running.remove(task)
            task["waits"] = len(step)
            running += [{"at": task["at"], "delay": task["delay"], "steps": p, "parent": task} for p in step]
        else:
            for engine, us in step:
                task["at"] = max(task["at"], free.get(engine, 0.0) if engine else 0.0) + us
                if engine:
                    free[engine] = task["at"]


def rope_tables():
    position = np.arange(S)
    inv = np.float32(1.0) / np.float32(10000.0) ** (np.arange(2, dtype=np.float32) / np.float32(2.0))
    cos, sin = [], []
    for at in (position // 16, position % 16):
        freq = at.astype(np.float32)[:, None] * inv
        cos += [np.cos(freq), np.cos(freq)]
        s = np.concatenate([np.sin(freq), np.sin(freq)], axis=1)
        s[:, 0::2] *= -1
        sin.append(s)
    return np.concatenate(cos + sin, axis=1).astype(np.float32)


def build(nc, x, ctx_in, mask, wq, bq, wk, bk, wv, bv, wo, bo, w_fc, router_w, router_b, lang_w, lang_b,
          w1, b1, w2, b2, rope, out):
    v, act, pe, pool, sp = nc.vector, nc.scalar, nc.tensor, nc.gpsimd, nc.sync
    rows = nc.dram_tensor("rows", [NT * P + P, D], F32, kind="Internal").ap()

    with ExitStack() as whole:
        def sb(name, shape, dt=F32, scope=whole):
            return scope.enter_context(nc.sbuf_tensor(name, shape, dt))

        def sem(name):
            return whole.enter_context(nc.semaphore(name))

        ident, identb = sb("ident", [P, P]), sb("identb", [P, P], BF16)
        upper, ones = sb("upper", [P, P]), sb("ones", [P, P])
        xs = sb("xs", [P, NT, D])
        attention = ExitStack()
        w1_sb0 = sb("w1_sb0", [P, E, F])
        weights = sb("weights", [P, E * F + E * FC * D])
        arena = Arena(weights, lambda name, shape, dt: sb(name, shape, dt, attention))
        w1_sb = [w1_sb0, weights[:, 0:E * F].rearrange("p (e f) -> p e f", e=E)]
        w2_sb = weights[:, E * F:].rearrange("p (e c d) -> p e c d", e=E, c=FC)
        logits = sb("logits", [P, NT, E + L])
        scratch = sb("scratch", [P, 1])

        s_const, s_setup = Steps(sem("const"), 0), Steps(sem("setup"), 0)
        s_x0, s_x1, s_x, s_qkv, s_small, s_w1, s_w2, s_zero = (
            sem(f"load_{w}") for w in ("x0", "x1", "x", "qkv", "small", "w1", "w2", "zero"))

        wqkv = arena("wqkv", [P, KC, 3 * D])
        wo_sb = sb("wo_sb", [P, KC, D], scope=attention)
        fc_in = sb("fc_in", [P, KC, D], scope=attention)
        fc_sb = sb("fc_sb", [P, KC, D], scope=attention)
        r_in = sb("r_in", [E + L, D], scope=attention)
        r_sb = sb("r_sb", [P, KC, E + L], scope=attention)
        r_bias = sb("r_bias", [P, E + L], scope=attention)
        bias_qkv = sb("bias_qkv", [P, 3 * D], scope=attention)
        bias_o = sb("bias_o", [P, D], scope=attention)
        table = sb("table", [P, T, 2, 8], scope=attention)
        cx = sb("cx", [P, T, D], scope=attention)
        mask_in = sb("mask_in", [NT, P], I32, scope=attention)
        mask_f = sb("mask_f", [NT, P], scope=attention)
        keep = sb("keep", [P, NT], scope=attention)
        keep_n = sb("keep_n", [P, T], scope=attention)
        drop = sb("drop", [P, NT], scope=attention)
        neg = sb("neg", [P, NT, PARTS], BF16, scope=attention)
        qk = arena("qk", [P, 2, T, D])
        xnT = arena("xnT", [P, KC, T, P])
        turn_a = sb("turn_a", [P, 2, T, H, 8], scope=attention)
        turn_b = sb("turn_b", [P, 2, T, H, 8], scope=attention)
        ctx_keep = sb("ctx_keep", [P, T, D], scope=attention)
        x_bias = sb("x_bias", [P, T, D], scope=attention)
        zeros = sb("zeros", [P, D], scope=attention)

        x_t = x.rearrange("b (t p) d -> p (b t) d", p=P)
        out_t = out[0:NT * P, :].rearrange("(t p) d -> p t d", p=P)
        rows_t = rows[0:NT * P, :].rearrange("(t p) d -> p t d", p=P)
        c_t = ctx_in.rearrange("b (t p) d -> p (b t) d", p=P)
        sp.dma_start(xs[:, 0:T, :], x_t[:, 0:T, :]).then_inc(s_x0, 16)
        for i, w in enumerate((wq, wk, wv)):
            sp.dma_start(wqkv[:, :, i * D:(i + 1) * D], w.rearrange("(c p) n -> p c n", p=P)).then_inc(s_qkv, 16)
        for i, b_ in enumerate((bq, bk, bv)):
            sp.dma_start(bias_qkv[:, i * D:(i + 1) * D],
                         b_.rearrange("(a d) -> a d", a=1).broadcast_to([P, D])).then_inc(s_qkv, 16)
        sp.dma_start(table[:, :, :, :], rope.rearrange("(t p) (a d) -> p t a d", p=P, a=2)).then_inc(s_qkv, 16)
        sp.dma_start(xs[:, T:2 * T, :], x_t[:, T:2 * T, :]).then_inc(s_x1, 16)
        sp.dma_start(bias_o[:, :], bo.rearrange("(a d) -> a d", a=1).broadcast_to([P, D])).then_inc(s_small, 16)
        sp.dma_start(r_bias[:, 0:E], router_b.rearrange("(a d) -> a d", a=1).broadcast_to([P, E])).then_inc(s_small, 16)
        sp.dma_start(r_bias[:, E:E + L], lang_b.rearrange("(a d) -> a d", a=1).broadcast_to([P, L])).then_inc(s_small, 16)
        sp.dma_start(wo_sb[:, :, :], wo.rearrange("(c p) n -> p c n", p=P)).then_inc(s_small, 16)
        sp.dma_start(fc_in[:, :, :], w_fc.rearrange("(c p) n -> p c n", p=P)).then_inc(s_small, 16)
        sp.dma_start(r_in[0:E, :], router_w).then_inc(s_small, 16)
        sp.dma_start(r_in[E:E + L, :], lang_w).then_inc(s_small, 16)
        sp.dma_start(mask_in[:, :], mask.rearrange("b a c (t p) -> (b a c t) p", p=P)).then_inc(s_small, 16)
        small = 8
        sp.wait_ge(s_qkv, 16 * 7)
        sp.wait_ge(s_x1, 16)
        sp.dma_start(xs[:, 2 * T:NT, :], x_t[:, 2 * T:NT, :]).then_inc(s_x, 16)
        for e in range(E):
            sp.dma_start(w1_sb[0][:, e, :], w1[e, 0:P, :]).then_inc(s_w1, 16)

        def load_w2(e):
            sp.dma_start(w2_sb[:, e, :, :], w2[e].rearrange("(c p) d -> p c d", p=P)).then_inc(s_w2, 16)


        s_const.done(pool.memset(ident[:, :], 0.0))
        s_const.done(pool.memset(upper[:, :], 1.0))
        s_const.wait(pool, 0)
        s_const.done(pool.affine_select(out=ident[:, :], in_=ident[:, :], compare_op=ALU.not_equal, fill=1.0,
                                        base=0, pattern=[[-1, P]], channel_multiplier=1))
        s_const.done(pool.affine_select(out=upper[:, :], in_=upper[:, :], compare_op=ALU.is_gt, fill=0.0,
                                        base=0, pattern=[[1, P]], channel_multiplier=-1))
        s_const.wait(pool, 0)
        s_const.done(pool.tensor_copy(identb[:, :], ident[:, :]))
        s_const.done(pool.memset(ones[:, :], 1.0))
        s_const.done(pool.memset(zeros[:, :], 0.0))

        turns = Turns(sem)
        banks = attention.enter_context(nc.psum_tensor("attention_psum", [P, 8, BANK], F32))
        ring = Ring(turns, "ring", [banks[:, i, :] for i in range(6)])
        a1 = Attention(nc, arena, turns, ring, "self", banks[:, 6, :], ident[:, :], identb[:, :], HD ** -0.5)
        early = arena.used // (FC * D) - E * F // (FC * D)
        a2 = Attention(nc, arena, turns, ring, "cross", banks[:, 7, :], ident[:, :], identb[:, :], 1.0 / D ** 0.5)
        ctx_load = turns.count("ctx_load", by=16)
        stored = turns.count("stored", by=16)
        for a in (a1, a2):
            a.setup(s_const)

        s_const.wait(act, 0)
        act.dma_start(rows[NT * P:NT * P + P, :], zeros[:, :]).then_inc(s_zero, 16)
        act.dma_start(out[NT * P:NT * P + P, :], zeros[:, :]).then_inc(s_zero, 16)

        for engine in (v, act, pe, pool):
            s_const.wait(engine, 0)
        act.activation(scratch[:, :], ones[:, 0:1], ACT.Exp)

        def residual(n):
            return xs[:, bass.ds(n * T, T), :]

        def setup():
            yield COST["lag_setup"]
            bank = a2.o_psum
            pe.wait_ge(s_small, 16 * small)
            for c in range(KC):
                for k in range(KC):
                    last = pe.transpose(bank[:, (c * KC + k) * P:(c * KC + k + 1) * P], fc_in[:, k, c * P:(c + 1) * P], ident[:, :])
            s_setup.done(last)
            s_setup.wait(v, 0)
            s_setup.done(v.tensor_copy(fc_sb[:, :, :].rearrange("p c n -> p (c n)"), bank))
            v.wait_ge(s_small, 16 * small)
            s_setup.done(v.tensor_scalar(mask_f[:, :], mask_in[:, :], 0.0, None, ALU.not_equal))
            s_setup.wait(pe, 0)
            for c in range(KC):
                pe.transpose(bank[:, c * (E + L):(c + 1) * (E + L)], r_in[:, c * P:(c + 1) * P], ident[0:E + L, 0:E + L])
            s_setup.done(pe.transpose(bank[:, 2 * BANK // 4:2 * BANK // 4 + NT], mask_f[:, :], ident[0:NT, 0:NT]))
            s_setup.wait(v, 0)
            s_setup.done(v.tensor_copy(r_sb[:, :, :].rearrange("p c n -> p (c n)"), bank[:, 0:KC * (E + L)]))
            s_setup.done(v.tensor_copy(keep[:, :], bank[:, 2 * BANK // 4:2 * BANK // 4 + NT]))
            s_setup.wait(v, 0)
            s_setup.done(v.tensor_scalar(drop[:, :], keep[:, :], -1.0, 1.0, ALU.mult, ALU.add))
            s_setup.wait(v, 0)
            for a, part in enumerate(bf16_parts(NEG)):
                s_setup.done(v.tensor_scalar(neg[:, :, a], drop[:, :], part, None, ALU.mult))
            for engine in (v, act, pe, pool):
                s_setup.wait(engine, 0)
            yield COST["setup"]

        def self_front(n, k):
            a = a1
            yield COST["lag_self_front"]
            yield from a.until((("split", 0), k - 1), (("split", 1), k - 1))
            for sequence, loaded in ((0, s_x0), (1, s_x1), (2, s_x)):
                if k == sequence:
                    v.wait_ge(loaded, 16)
            norm = yield from layer_norm(nc, a.dve, residual(n), a.xn[:, :, :], a.stats)
            yield from a.until((("v", T - 1), k - 1))
            turned = a.at["turned", k] = a.turn_rows(a.xn, xnT, [norm], [a.step(("v", t), k - 1) for t in range(T)])
            yield COST["turn"]
            if k == 0:
                for engine in (pe, v):
                    engine.wait_ge(s_qkv, 16 * 7)
            for t in range(T):
                i, bank = ring.fill(pe, turned)
                for c in range(KC):
                    last = pe.matmul(bank, xnT[:, c, t, :], wqkv[:, c, 0:2 * D], start=(c == 0), stop=(c == KC - 1))
                ring.filled(i, last)
                ring.take(v, i)
                added = ring.taken(i, v.tensor_tensor(
                    qk[:, :, t, :], bank.rearrange("p (w d) -> p w d", w=2),
                    bias_qkv[:, 0:2 * D].rearrange("p (w d) -> p w d", w=2), ALU.add))
                yield COST["qk"]
                after(v, added)
                part = qk[:, :, t, :].rearrange("p w (h d) -> p w h d", d=HD)[:, :, :, 4:12]
                cos = table[:, t, 0, :].rearrange("p (a b d) -> p a b d", a=1, b=1).broadcast_to([P, 2, H, 8])
                a.dve.done(v.tensor_tensor(turn_a[:, :, t], part, cos, ALU.mult))
                for z in range(2):
                    sin = table[:, t, 1, :].rearrange("p (a b d) -> p a b d", a=1, b=1)[:, :, :, z::2]
                    roped = a.dve.done(v.tensor_tensor(turn_b[:, :, t, :, z::2], part[:, :, :, 1 - z::2],
                                                       sin.broadcast_to([P, 2, H, 4]), ALU.mult))
                yield COST["rope"]
            part = qk[:, :, :, :].rearrange("p w t (h d) -> p w t h d", d=HD)[:, :, :, :, 4:12]
            after(v, roped)
            roped = a.dve.done(v.tensor_tensor(part.rearrange("p w t h d -> p (w t h) d"),
                                               turn_a[:, :, :, :, :].rearrange("p w t h d -> p (w t h) d"),
                                               turn_b[:, :, :, :, :].rearrange("p w t h d -> p (w t h) d"), ALU.add))
            yield COST["rope"]
            yield a.split(k, 0, qk[:, 0], roped), a.split(k, 1, qk[:, 1], roped)

        def self_early(n, k):
            a = a1
            yield from a.until((("split", 1), k), ("turned", k), ("half", k - 1))
            yield from a.stack_and_max(k, 0)
            yield from a.until(("o", k - 1))
            for t in range(T):
                i, bank = ring.fill(pe, a.step("turned", k))
                for c in range(KC):
                    last = pe.matmul(bank[:, 0:D], xnT[:, c, t, :], wqkv[:, c, 2 * D:3 * D],
                                     start=(c == 0), stop=(c == KC - 1))
                ring.filled(i, last)
                ring.take(v, i, a.step("o", k - 1))
                a.at[("v", t), k] = ring.taken(i, v.tensor_tensor(
                    a.v[:, t, :, 0:HD], bank[:, 0:D].rearrange("p (h d) -> p h d", d=HD),
                    bias_qkv[:, 2 * D:3 * D].rearrange("p (h d) -> p h d", d=HD), ALU.add))
                yield COST["v"]
            yield a.stack_and_max(k, 1), a.softmax_values(k, 0, COST["max_dma"])
            a.at["half", k] = a.o_moved

        def self_late(n, k):
            a = a1
            yield from a.until(("half", k), ("x", k - 1))
            yield from a.softmax_values(k, 1, COST["lag_half"])
            a.at["o", k] = a.o_moved
            after(pool, a.step("x", k - 1))
            pool.sem_inc(a.idle["pool"], 1)
            biased = a.pool.done(pool.tensor_tensor(
                x_bias[:, :, :], residual(n), bias_o[:, :].rearrange("p (a d) -> p a d", a=1)
                .broadcast_to([P, T, D]), ALU.add))
            i, bank = yield from a.outputs(k, wo_sb, a.step("o", k))
            ring.take(v, i, biased)
            a.at["x", k] = ring.taken(i, v.tensor_tensor(
                residual(n), bank.rearrange("p (t d) -> p t d", t=T), x_bias[:, :, :], ALU.add))
            yield COST["project"]
            a = a2
            yield from a.until((("split", 0), k - 1))
            norm = yield from layer_norm(nc, a.dve, residual(n), a.xn[:, :, :], a.stats, a1.step("x", k))
            yield from a.split(k, 0, a.xn[:, :, :], norm)

        def keys(n, k):
            a = a2
            yield COST["lag_keys"]
            yield from a1.until(("half", k))
            yield from a.until((("split", 1), k - 1), (("v", T - 1), k - 1), (("stacked", 1), k - 1))
            after(sp, a.step(("v", T - 1), k - 1))
            sp.sem_inc(a.idle["sp"], 1)
            loaded = ctx_load.done(sp.dma_start(cx[:, :, :], c_t[:, bass.ds(n * T, T), :]))
            after(pool, a.step(("stacked", 1), k - 1))
            pool.sem_inc(a.idle["pool"], 1)
            masks = a.pool.done(pool.tensor_copy(keep_n[:, :], keep[:, bass.ds(n * T, T)]))
            for t in range(T):
                masks = a.pool.done(pool.tensor_copy(a.parts[1][:, t, :, MASK0:MAX0],
                                                     neg[:, bass.ds(n * T + t, 1), :].broadcast_to([P, H, PARTS])))
            after(pool, masks, loaded)
            pool.sem_inc(a.idle["pool"], 1)
            for t in range(T):
                masked = a.pool.done(pool.tensor_scalar(ctx_keep[:, t, :], cx[:, t, :], keep_n[:, t:t + 1],
                                                        None, ALU.mult))
            yield COST["keys"]
            yield from a.split(k, 1, ctx_keep[:, :, :], masked)

        def cross_early(n, k):
            a = a2
            yield COST["lag_cross"]
            yield from a.until((("split", 0), k), (("split", 1), k), ("half", k - 1))
            yield from a.stack_and_max(k, 0)
            yield from a.until(("o", k - 1))
            after(pool, a.step(("split", 1), k), a.step("o", k - 1))
            pool.sem_inc(a.idle["pool"], 1)
            for t in range(T):
                a.at[("v", t), k] = a.pool.done(pool.tensor_copy(a.v[:, t, :, 0:HD],
                                                                 cx[:, t, :].rearrange("p (h d) -> p h d", d=HD)))
            yield a.stack_and_max(k, 1), a.softmax_values(k, 0, COST["max_dma"])
            a.at["half", k] = a.o_moved

        def cross_late(n, k):
            a = a2
            yield from a.until(("half", k), ("logits", k - 1))
            yield from a.softmax_values(k, 1, COST["lag_half"])
            a.at["o", k] = a.o_moved
            i, bank = yield from a.outputs(k, fc_sb, a.step("o", k))
            ring.take(v, i)
            summed = ring.taken(i, v.tensor_tensor(residual(n), bank.rearrange("p (t d) -> p t d", t=T),
                                                   residual(n), ALU.add))
            yield COST["project"]
            norm = yield from layer_norm(nc, a.dve, residual(n), a.ctx[:, :, :], a.stats_out, summed)
            after(sp, norm)
            stored.done(sp.dma_start(out_t[:, bass.ds(n * T, T), :], residual(n)))
            in_dram = stored.done(sp.dma_start(rows_t[:, bass.ds(n * T, T), :], a.ctx[:, :, :]))
            turned = a.turn_rows(a.ctx, a.ctxT, [norm])
            yield COST["turn"]
            i, bank = a.project(a.ctxT, r_sb, E + L, turned)
            ring.take(v, i, in_dram)
            a.at["logits", k] = ring.taken(i, v.tensor_tensor(
                logits[:, bass.ds(n * T, T), :], bank[:, 0:T * (E + L)].rearrange("p (t e) -> p t e", t=T),
                r_bias[:, :].rearrange("p (a e) -> p a e", a=1).broadcast_to([P, T, E + L]), ALU.add))
            yield COST["project"]

        delays = dict(COST["delays"])
        stages = [(stage, ahead, delays[stage.__name__]) for stage, ahead in (
            (self_early, 0), (cross_late, -3), (self_late, -1), (cross_early, -2), (keys, -1), (self_front, 1))]

        def weights_early():
            yield from a1.until(("x", B - 1 - turns.skipped))
            after(sp, a1.step("x", B - 1 - turns.skipped))
            for e in range(E + early):
                if e < E:
                    sp.dma_start(w1_sb[1][:, e, :], w1[e, P:2 * P, :]).then_inc(s_w1, 16)
                else:
                    load_w2(e - E)
                yield COST["load"]
                after(sp, a2.p_used[0])

        def turn(m, k):
            turns.begin()
            queue(*((delay, stage(m + ahead, k + ahead)) for stage, ahead, delay in stages))

        def part_turns(ms, *others):
            queue(*((delay, stage(m + ahead, m + ahead - turns.skipped)) for m in ms
                    for stage, ahead, delay in stages if 0 <= m + ahead < B), *((0.0, p) for p in others))

        full = range(3, B - 1)
        part_turns(range(-1, full[0]), setup())
        turn(full[0], full[0])
        turns.repeat(nc, full[1], full[-1] + 1, turn)
        part_turns(range(full[-1] + 1, B + 3), weights_early())

        for engine in (v, act, pe, pool, sp):
            after(engine, a2.step("logits", B - 1 - turns.skipped))
        attention.close()
        sp.wait_ge(s_zero, 16 * 2)
        experts(nc, whole, sem, scratch, out, rows, logits, ident, upper, ones, w1_sb, w2_sb, s_w1, s_w2, s_zero, b1, b2,
                lambda: [load_w2(e) for e in range(early, E)])


def route(nc, sb, sem, logits, upper, ones, bank):
    v, pe, pool, act = nc.vector, nc.tensor, nc.gpsimd, nc.scalar
    step = Steps(sem("route"), 0)

    def on(engine, instruction):
        step.done(instruction)
        step.wait(engine, 0)

    def tile(name, *shape, dt=F32):
        return sb(f"route_{name}", [P, *shape], dt)

    def last(ap, width):
        return ap.rearrange("p (t a) -> p t a", a=1).broadcast_to([P, NT, width])

    stat, recip = tile("stat", NT), tile("recip", NT)
    lang = tile("lang", NT, L + 1)
    z, prob = tile("z", NT, E), tile("prob", NT, E)
    hot = [tile(f"hot{i}", NT, E) for i in range(TOPK)]
    top = [tile(f"top{i}", NT) for i in range(TOPK)]
    gate = [tile(f"gate{i}", NT) for i in range(TOPK)]
    work, work2 = tile("work", NT, E), tile("work2", NT, E)
    order_i, order = tile("order_i", E, dt=I32), tile("order", E)
    index_i, index = tile("index_i", N_TILES, dt=I32), tile("index", N_TILES)
    slot_i, slot = tile("slot_i", P, dt=I32), tile("slot", P)
    lane_i, lane = tile("lane_i", 1, dt=I32), tile("lane", 1)
    start = tile("start", N_TILES)
    place, facts = tile("place", E, NT), tile("facts", E, NT, 3 + PARTS, dt=BF16)
    tile_expert = tile("tile_expert", N_TILES, dt=I32)

    on(pool, pool.iota(order_i[:, :], [[-1, E]], base=E, channel_multiplier=0))
    on(pool, pool.iota(index_i[:, :], [[1, N_TILES]], base=0, channel_multiplier=0))
    on(pool, pool.iota(slot_i[:, :], [[1, P]], base=0, channel_multiplier=0))
    on(v, pool.iota(lane_i[:, :], [[0, 1]], base=0, channel_multiplier=1))
    step.done(v.tensor_copy(lane[:, :], lane_i[:, :]))
    on(v, v.tensor_copy(index[:, :], index_i[:, :]))
    step.done(v.tensor_copy(slot[:, :], slot_i[:, :]))
    step.done(v.tensor_copy(order[:, :], order_i[:, :]))
    step.done(v.tensor_scalar(start[:, :], index[:, :], float(P), None, ALU.mult))
    step.done(v.memset(facts[:, :, :, 0], 1.0))
    step.done(v.tensor_copy(facts[:, :, :, 1], lane[:, :].rearrange("p (a b) -> p a b", a=1)
                        .broadcast_to([P, E, NT])))
    step.done(v.tensor_copy(facts[:, :, :, 2], index[:, 0:NT].rearrange("p (a b) -> p a b", a=1)
                        .broadcast_to([P, E, NT])))

    def softmax(src, width, out):
        on(v, v.tensor_reduce(stat[:, :], src, AXX, ALU.max))
        on(act, v.tensor_tensor(out, src, last(stat[:, :], width), ALU.subtract))
        on(v, act.activation(out, out, ACT.Exp))
        on(v, v.tensor_reduce(stat[:, :], out, AXX, ALU.add))
        on(v, v.reciprocal(recip[:, :], stat[:, :]))
        on(v, v.tensor_tensor(out, out, last(recip[:, :], width), ALU.mult))

    on(v, v.memset(lang[:, :, L:L + 1], 0.0))
    softmax(logits[:, :, E:E + L], L, lang[:, :, 0:L])
    on(v, v.tensor_tensor(work[:, :, 0:L], lang[:, :, 0:L], lang[:, :, 1:L + 1], ALU.add))
    for i in range(E // L):
        on(v, v.scalar_tensor_tensor(out=z[:, :, i * L:(i + 1) * L], in0=work[:, :, 0:L], scalar=0.1,
                                     in1=logits[:, :, i * L:(i + 1) * L], op0=ALU.mult, op1=ALU.add))
    softmax(z[:, :, :], E, prob[:, :, :])

    order_all = order[:, :].rearrange("p (a e) -> p a e", a=1).broadcast_to([P, NT, E])
    for i in range(TOPK):
        on(v, v.tensor_reduce(top[i][:, :], prob[:, :, :], AXX, ALU.max))
        on(v, v.tensor_tensor(work[:, :, :], prob[:, :, :], last(top[i][:, :], E), ALU.is_equal))
        on(v, v.tensor_tensor(work[:, :, :], work[:, :, :], order_all, ALU.mult))
        on(v, v.tensor_reduce(stat[:, :], work[:, :, :], AXX, ALU.max))
        on(v, v.tensor_tensor(hot[i][:, :, :], work[:, :, :], last(stat[:, :], E), ALU.is_equal))
        if i == 0:
            on(v, v.scalar_tensor_tensor(out=prob[:, :, :], in0=hot[0][:, :, :], scalar=-2.0,
                                         in1=prob[:, :, :], op0=ALU.mult, op1=ALU.add))
    on(v, v.tensor_tensor(work2[:, :, :], hot[0][:, :, :], hot[1][:, :, :], ALU.add))
    step.wait(pe, 0)

    chosen = work2[:, :, :].rearrange("p t e -> p (t e)")
    before, total = bank[:, 0:NT * E], bank[:, NT * E:2 * NT * E]
    pe.matmul(before, upper[:, :], chosen, start=True, stop=True)
    on(v, pe.matmul(total, ones[:, :], chosen, start=True, stop=True))

    on(v, v.tensor_tensor(stat[:, :], top[0][:, :], top[1][:, :], ALU.add))
    on(v, v.reciprocal(recip[:, :], stat[:, :]))
    for i in range(TOPK):
        step.done(v.tensor_tensor(gate[i][:, :], top[i][:, :], recip[:, :], ALU.mult))

    sums = [prob, z]
    step.done(v.tensor_copy(work2[:, :, :].rearrange("p t e -> p (t e)"), total))
    on(v, v.tensor_copy(sums[0][:, :, :].rearrange("p t e -> p (t e)"), total))
    for i, d in enumerate((1, 2, 4, 8)):
        a, b = sums[i % 2], sums[1 - i % 2]
        step.done(v.tensor_copy(b[:, 0:d, :], a[:, 0:d, :]))
        on(v, v.tensor_tensor(b[:, d:NT, :], a[:, d:NT, :], a[:, 0:NT - d, :], ALU.add))
    upto = sums[0]
    on(v, v.tensor_tensor(work2[:, :, :], upto[:, :, :], work2[:, :, :], ALU.subtract))

    fill_i, fill_i2 = tile("fill_i", E, dt=I32), tile("fill_i2", E, dt=I32)
    ends = [tile(f"ends{i}", E) for i in range(2)]
    tiles_of, start_row = tile("tiles_of", E), tile("start_row", E)
    on(v, v.tensor_scalar(fill_i[:, :], upto[:, NT - 1, :], float(P - 1), None, ALU.add))
    on(v, v.tensor_scalar(fill_i2[:, :], fill_i[:, :], P.bit_length() - 1, None, ALU.logical_shift_right))
    step.done(v.tensor_copy(tiles_of[:, :], fill_i2[:, :]))
    on(v, v.tensor_copy(ends[0][:, :], fill_i2[:, :]))
    for i, d in enumerate((1, 2, 4)):
        a, b = ends[i % 2], ends[1 - i % 2]
        step.done(v.tensor_copy(b[:, 0:d], a[:, 0:d]))
        on(v, v.tensor_tensor(b[:, d:E], a[:, d:E], a[:, 0:E - d], ALU.add))
    end = ends[1]
    on(v, v.tensor_tensor(start_row[:, :], end[:, :], tiles_of[:, :], ALU.subtract))
    on(v, v.tensor_scalar(start_row[:, :], start_row[:, :], float(P), None, ALU.mult))

    on(v, v.tensor_tensor(work2[:, :, :], work2[:, :, :], start_row[:, :]
                          .rearrange("p (a e) -> p a e", a=1).broadcast_to([P, NT, E]), ALU.add))
    on(v, v.tensor_tensor(work2[:, :, :].rearrange("p t e -> p (t e)"), before,
                          work2[:, :, :].rearrange("p t e -> p (t e)"), ALU.add))
    by_expert = work2[:, :, :].rearrange("p t e -> p e t")
    chosen_by = [x[:, :, :].rearrange("p t e -> p e t") for x in hot]
    on(v, v.tensor_scalar(work2[:, :, :], work2[:, :, :], 1.0, None, ALU.add))
    on(v, v.tensor_tensor(place[:, :, :], chosen_by[0], chosen_by[1], ALU.add))
    on(v, v.tensor_tensor(place[:, :, :], place[:, :, :], by_expert, ALU.mult))
    on(v, v.tensor_scalar(place[:, :, :], place[:, :, :], -1.0, None, ALU.add))

    for i in range(TOPK):
        on(v, v.tensor_tensor(hot[i][:, :, :], hot[i][:, :, :], last(gate[i][:, :], E), ALU.mult))
    on(v, v.tensor_tensor(work[:, :, :], hot[0][:, :, :], hot[1][:, :, :], ALU.add))
    rest = work[:, :, :].rearrange("p t e -> p e t")
    for a in range(PARTS):
        on(v, v.tensor_copy(facts[:, :, :, 3 + a], rest))
        if a + 1 < PARTS:
            on(v, v.tensor_tensor(rest, rest, facts[:, :, :, 3 + a], ALU.subtract))

    past = tile("past", N_TILES, E)
    on(v, v.tensor_tensor(past[:, :, :],
                          index[:, :].rearrange("p (j a) -> p j a", a=1).broadcast_to([P, N_TILES, E]),
                          end[:, :].rearrange("p (a e) -> p a e", a=1).broadcast_to([P, N_TILES, E]), ALU.is_ge))
    on(v, v.tensor_reduce(index[:, :], past[:, :, :], AXX, ALU.add))
    step.done(v.tensor_scalar(tile_expert[:, :], index[:, :], float(E - 1), None, ALU.min))
    return step, place, facts, tile_expert, start, slot, lane


def experts(nc, whole, sem, scratch, out, rows, logits, ident, upper, ones, w1_sb, w2_sb, s_w1, s_w2, s_zero, b1, b2,
            load_rest):
    v, act, pe, pool, sp = nc.vector, nc.scalar, nc.tensor, nc.gpsimd, nc.sync

    def sb(name, shape, dt=F32):
        return whole.enter_context(nc.sbuf_tensor(name, shape, dt))

    s_b, s_b2 = (sem(f"load_{w}") for w in ("b1", "b2"))
    b1_in, b1_sb = sb("b1_in", [E * FC, P]), sb("b1_sb", [P, E, FC])
    b2_sb = sb("b2_sb", [P, E, D])
    sp.dma_start(b1_in[:, :], b1.rearrange("e (c p) -> (e c) p", p=P)).then_inc(s_b, 16)
    load_rest()
    for e in range(E):
        sp.dma_start(b2_sb[:, e, :], b2[e:e + 1, :].broadcast_to([P, D])).then_inc(s_b2, 16)

    psum = whole.enter_context(nc.psum_tensor("experts_psum", [P, 7, BANK], F32))
    h_bank, hT_bank = (psum[:, b:b + 2, :].rearrange("p b n -> p (b n)") for b in (0, 2))
    x_bank, y_bank, fact_bank = psum[:, 4, :], psum[:, 5, :], psum[:, 6, :]

    step, place, facts, tile_expert, start, slot, lane = route(nc, sb, sem, logits, upper, ones, y_bank)
    s_bias = Steps(sem("bias"), 0)
    pe.wait_ge(s_b, 16)
    s_bias.done(pe.transpose(x_bank[:, 0:E * FC], b1_in[:, :], ident[0:E * FC, 0:E * FC]))
    act.activation(scratch[:, :], ones[:, 0:1], ACT.Gelu)
    s_bias.wait(v, 0)
    s_bias.done(v.tensor_copy(b1_sb[:, :, :].rearrange("p e c -> p (e c)"), x_bank[:, 0:E * FC]))

    beyond = sb("beyond", [P, 1])
    near, hit = sb("near", [P, NT]), sb("hit", [P, NT, P], BF16)
    found, spare, token_f = sb("found", [P, 3 + PARTS]), sb("spare", [P, 1]), sb("token_f", [P, 1])
    gate, gates = sb("gate", [P, 1]), sb("gates", [P, N_TILES])
    token, token_out, tokens = sb("token", [P, 1], I32), sb("token_out", [P, 1], I32), sb("tokens", [P, N_TILES], I32)
    x_rows, xT = sb("x_rows", [P, D]), sb("xT", [P, KC, P])
    hid, hidT, y, y_gated = sb("hid", [P, F]), sb("hidT", [P, FC, P]), sb("y", [P, D]), sb("y_gated", [P, D])
    (s_near, s_hit, s_fact, s_found, s_sum1, s_sum2, s_token, s_gather, s_turned_x, s_moved_x, s_up, s_moved_h,
     s_turned_h, s_gelu, s_down, s_moved_y, s_gated, s_add) = (
        Steps(sem(f"tile_{w}"), 1, by=16 if w in ("gather", "add") else 1) for w in
        ("near", "hit", "fact", "found", "sum1", "sum2", "token", "gather", "turned_x", "moved_x", "up", "moved_h",
         "turned_h", "gelu", "down", "moved_y", "gated", "add"))

    idle = sem("idle_tiles")

    def once(steps, instruction):
        steps.start()
        steps.done(instruction)

    def after(engine, steps, j):
        if not (isinstance(j, int) and j < 0):
            steps.wait(engine, j, 1)

    def expert_of(engine, j):
        return engine.value_load(tile_expert[0:1, bass.ds(j, 1)], min_val=0, max_val=E - 1)

    def hits(j):
        e = expert_of(v, j)
        once(s_near, v.tensor_scalar(near[:, :], place[:, bass.ds(e, 1), :].rearrange("p a t -> p (a t)"),
                                     start[:, bass.ds(j, 1)], None, ALU.subtract))
        after(v, s_near, j)
        after(v, s_fact, j - 1)
        once(s_hit, v.tensor_tensor(
            hit[:, :, :], slot[:, :].rearrange("p (a s) -> p a s", a=1).broadcast_to([P, NT, P]),
            near[:, :].rearrange("p (t a) -> p t a", a=1).broadcast_to([P, NT, P]), ALU.is_equal))

    def fact(j):
        e = expert_of(pe, j)
        after(pe, s_hit, j)
        after(pe, s_found, j - 1)
        for t in range(NT):
            last = pe.matmul(fact_bank[:, 0:3 + PARTS], hit[:, t, :],
                             facts[:, bass.ds(e, 1), t, :].rearrange("p a c -> p (a c)"),
                             start=(t == 0), stop=(t == NT - 1))
        once(s_fact, last)
        after(v, s_fact, j)
        once(s_found, v.tensor_copy(found[:, :], fact_bank[:, 0:3 + PARTS]))
        after(v, s_found, j)
        v.scalar_tensor_tensor(out=token_f[:, :], in0=found[:, 2:3], scalar=float(P), in1=found[:, 1:2],
                               op0=ALU.mult, op1=ALU.add)
        v.tensor_scalar(spare[:, :], found[:, 0:1], -1.0, 1.0, ALU.mult, ALU.add)
        once(s_sum1, v.tensor_tensor(gate[:, :], found[:, 3:4], found[:, 4:5], ALU.add))
        after(v, s_sum1, j)
        once(s_sum2, v.tensor_tensor(spare[:, :], spare[:, :], beyond[:, :], ALU.mult))
        after(v, s_sum2, j)
        after(v, s_gather, j - 1)
        v.tensor_tensor(tokens[:, bass.ds(j, 1)], token_f[:, :], spare[:, :], ALU.add)
        v.tensor_tensor(gates[:, bass.ds(j, 1)], gate[:, :], found[:, 5:6], ALU.add)
        once(s_token, v.tensor_tensor(token[:, :], token_f[:, :], spare[:, :], ALU.add))

    def gather(j):
        after(pool, s_token, j)
        after(pool, s_turned_x, j - 1)
        pool.sem_inc(idle, 1)
        once(s_gather, pool.indirect_dma_start(
            out=x_rows[:, :], out_offset=None, in_=rows,
            in_offset=bass.IndirectOffsetOnAxis(ap=token[:, :].bitcast(U32), axis=0)))

    def turn_x(j):
        after(pe, s_gather, j)
        after(pe, s_moved_x, j - 1)
        for c in range(KC):
            last = pe.transpose(x_bank[:, c * P:(c + 1) * P], x_rows[:, c * P:(c + 1) * P], ident[:, :])
        once(s_turned_x, last)
        after(act, s_turned_x, j)
        after(act, s_up, j - 1)
        once(s_moved_x, act.copy(xT[:, :, :].rearrange("p c t -> p (c t)"), x_bank[:, 0:D]))

    def up_layer(j):
        e = expert_of(pe, j)
        after(pe, s_moved_x, j)
        after(pe, s_moved_h, j - 1)
        for half in range(F // BANK):
            for c in range(KC):
                last = pe.matmul(h_bank[:, half * BANK:(half + 1) * BANK], xT[:, c, :],
                                 w1_sb[c][:, bass.ds(e, 1), half * BANK:(half + 1) * BANK]
                                 .rearrange("p a n -> p (a n)"), start=(c == 0), stop=(c == KC - 1))
        once(s_up, last)
        after(v, s_up, j)
        after(v, s_turned_h, j - 1)
        once(s_moved_h, v.tensor_copy(hid[:, :], h_bank))

    def turn_h(j):
        after(pe, s_moved_h, j)
        after(pe, s_gelu, j - 1)
        for c in range(FC):
            last = pe.transpose(hT_bank[:, c * P:(c + 1) * P], hid[:, c * P:(c + 1) * P], ident[:, :])
        once(s_turned_h, last)
        e = expert_of(act, j)
        after(act, s_turned_h, j)
        after(act, s_down, j - 1)
        for c in range(FC):
            last = act.activation(hidT[:, c, :], hT_bank[:, c * P:(c + 1) * P], ACT.Gelu,
                                  bias=b1_sb[:, bass.ds(e, 1), c])
        once(s_gelu, last)

    def down_layer(j):
        e = expert_of(pe, j)
        after(pe, s_gelu, j)
        after(pe, s_moved_y, j - 1)
        for c in range(FC):
            last = pe.matmul(y_bank[:, 0:D], hidT[:, c, :],
                             w2_sb[:, bass.ds(e, 1), c, :].rearrange("p a n -> p (a n)"),
                             start=(c == 0), stop=(c == FC - 1))
        once(s_down, last)
        e = expert_of(v, j)
        after(v, s_down, j)
        after(v, s_gated, j - 1)
        once(s_moved_y, v.tensor_tensor(y[:, :], y_bank[:, 0:D],
                                        b2_sb[:, bass.ds(e, 1), :].rearrange("p a n -> p (a n)"), ALU.add))
        after(v, s_moved_y, j)
        after(v, s_add, j - 1)
        v.tensor_copy(token_out[:, :], tokens[:, bass.ds(j, 1)])
        once(s_gated, v.tensor_scalar(y_gated[:, :], y[:, :], gates[:, bass.ds(j, 1)], None, ALU.mult))
        after(pool, s_gated, j)
        pool.sem_inc(idle, 1)
        once(s_add, pool.indirect_dma_start(
            out=out, out_offset=bass.IndirectOffsetOnAxis(ap=token_out[:, :].bitcast(U32), axis=0),
            in_=y_gated[:, :], in_offset=None, compute_op=ALU.add))

    on_start = Steps(sem("tiles_start"), 0)
    step.wait(v, 0)
    on_start.done(v.tensor_scalar(beyond[:, :], lane[:, :], float(NT * P), None, ALU.add))
    for engine in (v, act, pe, pool):
        step.wait(engine, 0)
        s_bias.wait(engine, 0)
        on_start.wait(engine, 0)
    pool.wait_ge(s_zero, 16 * 2)

    def tick(j):
        steady = (fact, 3), (turn_h, 0), (hits, 4), (up_layer, 1), (gather, 3), (turn_x, 2), (down_layer, 0)
        first = (turn_h, 0), (up_layer, 1), (fact, 3), (gather, 3), (hits, 4), (turn_x, 2), (down_layer, 0)
        for what, ahead in first if isinstance(j, int) and j < 1 else steady:
            if not isinstance(j, int) or 0 <= j + ahead < N_TILES:
                what(j + ahead)

    for j in range(-4, -1):
        tick(j)
    pe.wait_ge(s_w1, 16 * KC * E)
    tick(-1)
    pe.wait_ge(s_w2, 16 * E)
    v.wait_ge(s_b2, 16 * E)
    tick(0)
    with nc.Fori(1, N_TILES - 4) as j:
        tick(j)
    for j in range(N_TILES - 4, N_TILES):
        tick(j)
    s_add.wait(pool, N_TILES - 1, 1)


_INS = ["x", "ctx_1024", "mask_Bx1x1xS2_ik0", "L0_attn_Wq", "L0_attn_bq", "L0_attn_Wk", "L0_attn_bk",
        "L0_attn_Wv", "L0_attn_bv", "L0_attn_Wo", "L0_attn_bo", "L0_xattn_W_fc", "L0_ffn_router_w",
        "L0_ffn_router_b", "L0_ffn_lang_w", "L0_ffn_lang_b", "L0_ffn_w1", "L0_ffn_b1", "L0_ffn_w2",
        "L0_ffn_b2"]


def kernel(**inputs):
    import concourse.bacc as bacc
    from concourse.bass_utils import run_bass_kernel_spmd

    nc = bacc.Bacc("TRN2", target_bir_lowering=False, num_devices=1)
    arrays = {f"in_{name}": np.ascontiguousarray(inputs[name]) for name in _INS}
    arrays["rope"] = rope_tables()
    args = [nc.dram_tensor(name, a.shape, mybir.dt.from_np(a.dtype), kind="ExternalInput").ap()
            for name, a in arrays.items()]
    out = nc.dram_tensor("out", (B * S + P, D), F32, kind="ExternalOutput").ap()
    build(nc, *args, out)
    r = run_bass_kernel_spmd(nc, [arrays], core_ids=[0])
    return r.results[0]["out"][:B * S].reshape(B, S, D)
```
